# Optimizing a Trainium2 kernel written in Bass

```python
import numpy as np
import jax
import jax.numpy as jnp

def _softmax(x, axis=-1):
    return jax.nn.softmax(x, axis=axis)

def _gelu(x):
    return jax.nn.gelu(x, approximate=True)

def _silu(x):
    return jax.nn.silu(x)

def _sigmoid(x):
    return jax.nn.sigmoid(x)

def _layernorm(x, axis=-1, eps=1e-05):
    m = jnp.mean(x, axis=axis, keepdims=True)
    v = jnp.var(x, axis=axis, keepdims=True)
    return (x - m) / jnp.sqrt(v + eps)

def _scatter_add(tgt, idx, src, axis=0):
    return tgt.at[idx].add(src)

def _segment_sum(src, seg, n):
    return jax.ops.segment_sum(src, seg, n)
kernel_name = 'mk_cond_resid_d4_seqx_r8_13f0e5'

def setup_inputs(seed: int=0):
    np.random.seed(seed)
    _w = jnp.asarray

    def _rec_inputs():
        import jax
        import jax.numpy as jnp
        _rk = jax.random.key(seed)
        x = 7.22e-05 + 1 * jax.random.normal(jax.random.fold_in(_rk, 1), (64, 32, 512), jnp.float32)
        _lenS = 32 - jax.random.randint(jax.random.fold_in(_rk, 7), (64,), 0, max(1, 32 // 4) + 1, jnp.int32)
        _lenS2 = 32 - jax.random.randint(jax.random.fold_in(_rk, 8), (64,), 0, max(1, 32 // 4) + 1, jnp.int32)
        itok_B_2_6 = jax.random.randint(jax.random.fold_in(_rk, 11), (64,), 2, 7, jnp.int32)
        itok_B_0_15 = jax.random.randint(jax.random.fold_in(_rk, 12), (64,), 0, 16, jnp.int32)
        itok_B_0_7 = jax.random.randint(jax.random.fold_in(_rk, 13), (64,), 0, 8, jnp.int32)
        return (x, itok_B_2_6, itok_B_0_15, itok_B_0_7)
    x, itok_B_2_6, itok_B_0_15, itok_B_0_7 = _rec_inputs()

    def _L0_cond_setup():
        import jax, jax.numpy as jnp
        import numpy as np
        B, N, H, F = (4, 64, 512, 1376)
        L, R, RANK = (1, 16, 16)
        SCALE = 0.5
        key = jax.random.key(seed)
        ks = jax.random.split(key, 12)
        nrm = lambda k, shape, fan: jax.random.normal(k, shape, jnp.float32) * fan ** (-0.5)
        inp = {'x': jax.random.normal(ks[0], (B, N, H), jnp.float32), 'W_gate': nrm(ks[1], (F, H), H), 'W_up': nrm(ks[2], (F, H), H), 'W_down': nrm(ks[3], (H, F), F), 'A_gate': nrm(ks[4], (L, R, RANK, H), H), 'B_gate': nrm(ks[5], (L, R, F, RANK), RANK), 'A_up': nrm(ks[6], (L, R, RANK, H), H), 'B_up': nrm(ks[7], (L, R, F, RANK), RANK), 'A_down': nrm(ks[8], (L, R, RANK, F), F), 'B_down': nrm(ks[9], (L, R, H, RANK), RANK), 'lora_indices': jax.random.randint(ks[10], (B,), 0, R), 'layer_idx': 0}
        return inp
    _L0_cond_all = _L0_cond_setup()
    _L0_cond_in = {k: v for k, v in _L0_cond_all.items() if k in ('W_gate', 'W_up', 'W_down', 'A_gate', 'B_gate', 'A_up', 'B_up', 'A_down', 'B_down')}
    del _L0_cond_all

    def _L1_cond_setup():
        import jax, jax.numpy as jnp
        import numpy as np
        B, C, T = (64, 32, 512)
        S, D = (16, 32)
        key = jax.random.key(seed)
        k1, k2, k3 = jax.random.split(key, 3)
        x = jax.random.normal(k1, (B, C, T), dtype=jnp.float32)
        condition = jax.random.randint(k2, (B,), 0, S, dtype=jnp.int64)
        bound = float(np.sqrt(6.0 / C))
        weights = jax.random.uniform(k3, (S, C, D), dtype=jnp.float32, minval=-bound, maxval=bound)
        return {'x': x, 'condition': condition, 'weights': weights}
    _L1_cond_all = _L1_cond_setup()
    _L1_cond_in = {k: v for k, v in _L1_cond_all.items() if k in ('weights',)}
    del _L1_cond_all

    def _L2_cond_setup():
        import jax, jax.numpy as jnp
        import numpy as np
        TOP_K = 2
        LANG_BIAS = 5.0
        SCALING = 32.0 / 16.0
        LANGUAGE_PAD_ID = -1
        key = jax.random.key(seed)
        ks = jax.random.split(key, 6)
        B, T, D, O, E, R = (4, 256, 512, 512, 8, 16)
        x = jax.random.normal(ks[0], (B, T, D), dtype=jnp.float32)
        language_ids = jax.random.randint(ks[1], (B,), 0, E).astype(jnp.int64)
        W = jax.random.normal(ks[2], (O, D), dtype=jnp.float32) * (1.0 / np.sqrt(D))
        Wr = jax.random.normal(ks[3], (E, D), dtype=jnp.float32) * (1.0 / np.sqrt(D))
        A = jax.random.normal(ks[4], (E, R, D), dtype=jnp.float32) * (1.0 / np.sqrt(D))
        Bm = jax.random.normal(ks[5], (O, R), dtype=jnp.float32) * 0.0
        Bm = jnp.broadcast_to(Bm, (E, O, R)) + jax.random.normal(ks[5], (E, O, R), dtype=jnp.float32) * 0.02
        return {'x': x, 'language_ids': language_ids, 'W': W, 'Wr': Wr, 'A': A, 'B': Bm}
    _L2_cond_all = _L2_cond_setup()
    _L2_cond_in = {k: v for k, v in _L2_cond_all.items() if k in ('W', 'Wr', 'A', 'B')}
    del _L2_cond_all

    def _L3_cond_setup():
        import jax, jax.numpy as jnp
        import numpy as np
        NUM_CONDITIONS = 16
        IN_CH = 32
        OUT_CH = 32
        B = 64
        T = 512
        key = jax.random.key(seed)
        k_x, k_w, k_c = jax.random.split(key, 3)
        x = jax.random.normal(k_x, (B, IN_CH, T), dtype=jnp.float32)
        bound = float(np.sqrt(6.0 / IN_CH))
        weights = jax.random.uniform(k_w, (NUM_CONDITIONS, IN_CH, OUT_CH), dtype=jnp.float32, minval=-bound, maxval=bound)
        condition = jax.random.randint(k_c, (B,), 0, NUM_CONDITIONS, dtype=jnp.int64)
        return {'x': x, 'weights': weights, 'condition': condition}
    _L3_cond_all = _L3_cond_setup()
    _L3_cond_in = {k: v for k, v in _L3_cond_all.items() if k in ('weights',)}
    del _L3_cond_all
    return {'x': x, 'itok_B_2_6': itok_B_2_6, 'itok_B_0_15': itok_B_0_15, 'itok_B_0_7': itok_B_0_7, 'L0_cond_W_gate': _L0_cond_in['W_gate'], 'L0_cond_W_up': _L0_cond_in['W_up'], 'L0_cond_W_down': _L0_cond_in['W_down'], 'L0_cond_A_gate': _L0_cond_in['A_gate'], 'L0_cond_B_gate': _L0_cond_in['B_gate'], 'L0_cond_A_up': _L0_cond_in['A_up'], 'L0_cond_B_up': _L0_cond_in['B_up'], 'L0_cond_A_down': _L0_cond_in['A_down'], 'L0_cond_B_down': _L0_cond_in['B_down'], 'L1_cond_weights': _L1_cond_in['weights'], 'L2_cond_W': _L2_cond_in['W'], 'L2_cond_Wr': _L2_cond_in['Wr'], 'L2_cond_A': _L2_cond_in['A'], 'L2_cond_B': _L2_cond_in['B'], 'L3_cond_weights': _L3_cond_in['weights']}

def reference(x, itok_B_2_6, itok_B_0_15, itok_B_0_7, L0_cond_W_gate, L0_cond_W_up, L0_cond_W_down, L0_cond_A_gate, L0_cond_B_gate, L0_cond_A_up, L0_cond_B_up, L0_cond_A_down, L0_cond_B_down, L1_cond_weights, L2_cond_W, L2_cond_Wr, L2_cond_A, L2_cond_B, L3_cond_weights):
    import jax
    import jax.numpy as jnp

    def _L0_cond_ref(x, W_gate, W_up, W_down, A_gate, B_gate, A_up, B_up, A_down, B_down, lora_indices, layer_idx):
        import jax, jax.numpy as jnp
        import numpy as np
        B, N, H, F = (4, 64, 512, 1376)
        L, R, RANK = (1, 16, 16)
        SCALE = 0.5

        def lora_add(base, inp, A, B):
            Ab = A[layer_idx][lora_indices]
            Bb = B[layer_idx][lora_indices]
            t = jnp.einsum('bri,bni->bnr', Ab, inp)
            return base + jnp.einsum('bor,bnr->bno', Bb, t) * SCALE
        gate = lora_add(jnp.einsum('bnh,fh->bnf', x, W_gate), x, A_gate, B_gate)
        up = lora_add(jnp.einsum('bnh,fh->bnf', x, W_up), x, A_up, B_up)
        act = jax.nn.silu(gate) * up
        down = lora_add(jnp.einsum('bnf,hf->bnh', act, W_down), act, A_down, B_down)
        return down

    def _L1_cond_ref(x, condition, weights):
        import jax, jax.numpy as jnp
        import numpy as np
        B, C, T = (64, 32, 512)
        S, D = (16, 32)
        W = weights[condition]
        return jnp.einsum('bct,bcd->bdt', x, W)

    def _L2_cond_ref(x, language_ids, W, Wr, A, B):
        import jax, jax.numpy as jnp
        import numpy as np
        TOP_K = 2
        LANG_BIAS = 5.0
        SCALING = 32.0 / 16.0
        LANGUAGE_PAD_ID = -1
        base = jnp.einsum('btd,od->bto', x, W)
        E = Wr.shape[0]
        logits = jnp.einsum('btd,ed->bte', x.astype(jnp.float32), Wr.astype(jnp.float32))
        expert_targets = language_ids
        valid = expert_targets >= 0
        tgt = jnp.where(valid, expert_targets, 0)
        bias = jax.nn.one_hot(tgt, E, dtype=logits.dtype) * LANG_BIAS
        bias = jnp.where(valid[:, None], bias, 0.0)
        logits = logits + bias[:, None, :]
        topw, topi = jax.lax.top_k(logits, TOP_K)
        weights = jax.nn.softmax(topw, axis=-1)
        gates = jnp.sum(jax.nn.one_hot(topi, E, dtype=weights.dtype) * weights[..., None], axis=-2)
        gates = gates.astype(x.dtype)
        h = jnp.einsum('btd,erd->bter', x, A)
        lora_out = jnp.einsum('bter,bte,eor->bto', h, gates, B)
        return base + SCALING * lora_out

    def _L3_cond_ref(x, weights, condition):
        import jax, jax.numpy as jnp
        import numpy as np
        NUM_CONDITIONS = 16
        IN_CH = 32
        OUT_CH = 32
        B = 64
        T = 512
        W = weights[condition]
        return jnp.einsum('bct,bcd->bdt', x, W)
    x = x + _L0_cond_ref(x, L0_cond_W_gate, L0_cond_W_up, L0_cond_W_down, L0_cond_A_gate, L0_cond_B_gate, L0_cond_A_up, L0_cond_B_up, L0_cond_A_down, L0_cond_B_down, itok_B_2_6, 0)
    x = x + _L1_cond_ref(x, itok_B_0_15, L1_cond_weights)
    x = x + _L2_cond_ref(x, itok_B_0_7, L2_cond_W, L2_cond_Wr, L2_cond_A, L2_cond_B)
    x = x + _L3_cond_ref(x, L3_cond_weights, itok_B_0_15)
    return x

_drawn_inputs = setup_inputs


def setup_inputs(seed=0):
    import zlib

    import numpy as np

    out = dict(_drawn_inputs(seed))
    spreads = {}
    factors = {}
    for name, (base, spread) in spreads.items():
        noise = np.random.default_rng([zlib.crc32(name.encode()), seed]).standard_normal(out[name].shape)
        drawn = base * np.exp(spread * noise) if base else spread * noise
        out[name] = jnp.asarray(drawn.astype(out[name].dtype))
    for name, factor in factors.items():
        out[name] = (out[name] * factor).astype(out[name].dtype)
    return out
```

```python
from contextlib import ExitStack

import numpy as np

import concourse.bass as bass
from concourse import mybir

F32 = mybir.dt.float32
F32R = mybir.dt.float32r
I32 = mybir.dt.int32
U32 = mybir.dt.uint32
ALU = mybir.AluOpType
ACT = mybir.ActivationFunctionType
AX_X = mybir.AxisListType.X

P = 128
BATCHES, CH, H = 64, 32, 512
F = 1376
RANK = 16
ADAPTERS = 16
CONDS = 16
EXPERTS = 8
LORA_SCALE = 0.5
LANG_BIAS = 5.0
SCALING = 2.0

ROWS = BATCHES * CH
HC = H // P
GROUP = 256
NG = ROWS // GROUP
QUADS = GROUP // P
NT = ROWS // P
QB = P // CH
HALF = QB * RANK
FC = -(-F // P)
LASTW = F - (FC - 1) * P
STEPS = NG * FC
AD_PIECES = [(0, 4), (4, 8), (8, FC)]
GATHERED = ("b", "bd", "agu", "ad")
RING = 5
BD = 6
RA = EXPERTS + EXPERTS * RANK


def cw(c):
    return P if c < FC - 1 else LASTW


CONST_COLS = {}


def const_array():
    p = np.arange(P)
    blocks = {
        "ident": np.eye(P),
        "mask": LORA_SCALE * ((p[:, None] % HALF) // RANK == p[None, :] // CH),
        "is_quad": (p[:, None] % HALF) // RANK == np.arange(QB)[None, :],
        "is_oct": p[:, None] // RANK == np.arange(P // RANK)[None, :],
        "is_tok": p[:, None] // CH == np.arange(QB)[None, :],
        "row_gu": (p % RANK + ADAPTERS * RANK * (p // HALF))[:, None],
        "row_rank": (p % RANK)[:, None],
        "row_ch": (p % CH)[:, None],
        "iota": np.broadcast_to(np.arange(EXPERTS), (P, EXPERTS)),
    }
    at = 0
    for name, b in blocks.items():
        CONST_COLS[name] = (at, at + b.shape[1])
        at += b.shape[1]
    return np.concatenate([b.astype(np.float32) for b in blocks.values()], axis=1)


CONSTS = const_array()


def staged_items(s):
    g, f = divmod(s, FC)
    if s < 0:
        return [("x", 0, 0), ("wgu", 0, 0), ("x", 0, 1), ("wgu", 0, 1), ("agu", 0, 0), ("agu", 0, 1),
                ("b", 0), ("wgu", 1, 0), ("wgu", 1, 1), ("b", 1), ("wd", 0), ("ad", 0, 0)]
    out = []
    if g == 0 and f + 2 < FC:
        out += [("wgu", f + 2, 0), ("wgu", f + 2, 1)]
    if s + 2 < STEPS:
        out.append(("b", s + 2))
    if g == 0 and f + 1 < FC:
        out.append(("wd", f + 1))
    if g == 0:
        out += {0: [("ad", 0, 1)], 2: [("ad", 0, 2)]}.get(f, [])
    elif f == 0:
        out.append(("ad", g, 2))
    if g + 1 < NG:
        n = g + 1
        out += {0: [("x", n, 0)], 1: [("x", n, 1), ("agu", n, 0)], 3: [("agu", n, 1)],
                4: [("ad", n, 0)], 8: [("ad", n, 1)]}.get(f, [])
    out += {6: [("bd", g, 0)], 7: [("bd", g, 1)]}.get(f, [])
    return out


def pe_side(s):
    g, f = divmod(s, FC)
    out = []
    if g == 0:
        out += {0: [("adt", 0, 0)], 1: [("adt", 0, 1)], 3: [("adt", 0, 2)]}.get(f, [])
    elif f == 0:
        out.append(("adt", g, 2))
    if g + 1 < NG:
        n = g + 1
        out += {2: [("at", n, 0)], 3: [("tg", n, 0)], 4: [("at", n, 1)], 5: [("tg", n, 1), ("adt", n, 0)],
                9: [("adt", n, 1)]}.get(f, [])
    return out


def lane_jobs(s):
    g, f = divmod(s, FC)
    if s < 0:
        jobs = []
        for item in staged_items(-1):
            if item[0] == "agu":
                if item[2] == 1:
                    jobs += [("at", 0, 0), ("at", 0, 1), ("t", 0)]
            elif item[0] != "ad":
                jobs.append(item)
        return jobs
    jobs = []
    if f == 1 and g > 0:
        jobs.append(("x1", g - 1))
    if s < STEPS:
        jobs.append(("act", s))
    if f == 0 and g > 0:
        jobs.append(("td", g - 1))
    if s >= STEPS:
        return jobs
    jobs += [j for j in pe_side(s) if j[0] in ("adt", "at")]
    if f == 6 and g + 1 < NG:
        jobs.append(("t", g + 1))
    jobs += [j for j in staged_items(s) if j[0] not in ("agu", "ad")]
    return jobs


def bass_conditioned_residual_chain(nc, x_t, x_rows, it_lora, it_cond, it_lang, wgu, wd, a_gu, b_d, w13,
                                    w2_t, ra_t, b2, consts, *rest):
    b_gu, rest = rest[:FC], rest[FC:]
    a_d, rest = rest[:len(AD_PIECES)], rest[len(AD_PIECES):]
    (out,) = rest

    items = [it for s in range(-1, STEPS) for it in staged_items(s)]
    item_no = {it: n for n, it in enumerate(items)}
    item_dmas = {it: QUADS if it[0] == "b" else 1 for it in items}
    arrived = {}
    total = {}
    for n, it in enumerate(items):
        own = (it[0] in GATHERED, n % RING)
        total[own] = total.get(own, 0) + 16 * item_dmas[it]
        arrived[it] = total[own]
    pairs = [j for s in range(-1, STEPS + FC) for j in lane_jobs(s) if j[0] != "x1"]
    pair_no = {j: n + 1 for n, j in enumerate(pairs)}
    pe_read = [it for it in items if it[0] in ("agu", "ad")]
    pe_tr = [("agu", 0, 0), ("agu", 0, 1)] + [
        ({"at": "agu", "adt": "ad"}[j[0]],) + j[1:] for s in range(STEPS) for j in pe_side(s) if j[0] != "tg"]
    tr_no = {it: n + 1 for n, it in enumerate(pe_tr)}

    with ExitStack() as ctx:
        def sb(name, shape, dt=F32, stack=ctx):
            return stack.enter_context(nc.sbuf_tensor(name, [P, *shape], dt))

        def ps(name, shape, stack=ctx):
            return stack.enter_context(nc.psum_tensor(name, [P, *shape], F32))

        def sem(name):
            return ctx.enter_context(nc.semaphore(name))

        const_sb = sb("const_sb", [CONSTS.shape[1]])
        itok = sb("itok", [3, BATCHES], I32)
        picked = sb("picked", [BATCHES])
        sel = sb("sel", [4, NT])
        idx_gu = sb("idx_gu", [NT], U32)
        idx_dup = sb("idx_dup", [NT], U32)
        idx_oct = sb("idx_oct", [NG], U32)
        idx_tok = sb("idx_tok", [NT], U32)
        x_scratch = nc.dram_tensor("x_after_l0", [ROWS, H], F32, kind="Internal").ap()

        def const(name):
            a, b = CONST_COLS[name]
            return const_sb[:, a:b]

        ident = const("ident")

        mem_a = ExitStack()
        wgu_sb = sb("wgu_sb", [(FC - 1) * 4 * H + 4 * HC * LASTW], F32R, mem_a)
        wd_sb = sb("wd_sb", [FC, 2, H], F32R, mem_a)
        ring = sb("ring", [RING, H], F32, mem_a)
        xt = sb("xt", [2, HC, 2, GROUP], F32R, mem_a)
        act = sb("act", [2, GROUP], F32, mem_a)
        act_hl = sb("act_hl", [2, 2, GROUP], F32R, mem_a)
        b_sel = sb("b_sel", [2, QUADS * 2 * P], F32R, mem_a)
        agu_t = sb("agu_t", [2, HC, P], F32R, mem_a)
        ad_t = sb("ad_t", [FC, QUADS, 2, HALF], F32R, mem_a)
        t_raw = sb("t_raw", [GROUP], F32, mem_a)
        t_hl = sb("t_hl", [2, 2, 2, GROUP], F32R, mem_a)
        td_raw = sb("td_raw", [GROUP], F32, mem_a)
        td_hl = sb("td_hl", [2, GROUP], F32R, mem_a)
        bd_hl = sb("bd_hl", [QUADS, 2, H], F32R, mem_a)
        x_res = sb("x_res", [QUADS, H], F32, mem_a)
        mem_a.close()

        banks_a = ExitStack()
        gu_ps = [ps(f"gu_ps{i}", [2, GROUP], banks_a) for i in range(2)]
        down_ps = [ps(f"down_ps{i}", [H], banks_a) for i in range(QUADS)]
        td_ps = ps("td_ps", [2, GROUP], banks_a)
        tg_ps = ps("tg_ps", [2, GROUP], banks_a)
        tr_gu_ps = ps("tr_gu_ps", [HC, P], banks_a)
        tr_d_ps = ps("tr_d_ps", [4, P], banks_a)
        banks_a.close()

        mem_b = ctx
        w_raw = sb("w_raw", [HC * H + HC * RA + H])
        w13_raw = sb("w13_raw", [NT, 2 * CH])
        x1 = sb("x1", [2, H])
        w2_hl = sb("w2_hl", [2, HC, H], F32R)
        ra_hl = sb("ra_hl", [2, HC, RA], F32R)
        b2_hl = sb("b2_hl", [2, H], F32R)
        lang5 = sb("lang5", [NT, EXPERTS])
        bd_raw = sb("bd_raw", [2, 2, P])
        bd13_hl = sb("bd13_hl", [BD, 2, 2, P], F32R)
        x1_hl = sb("x1_hl", [2, 2, H], F32R)
        x2 = sb("x2", [3, H])
        x2t_hl = sb("x2t_hl", [2, 2, HC, P], F32R)
        route = sb("route", [2, 64])
        order = sb("order", [2, EXPERTS], U32)
        hg = sb("hg", [2, P])
        hgt_hl = sb("hgt_hl", [2, 2, P], F32R)
        x3 = sb("x3", [3, H])
        x3_hl = sb("x3_hl", [2, 2, H], F32R)
        y = sb("y", [2, H])

        base_ps = [ps(f"base_ps{i}", [H]) for i in range(2)]
        ra_ps = [ps(f"ra_ps{i}", [H]) for i in range(2)]
        l1_ps = ps("l1_ps", [H])
        x2t_ps = ps("x2t_ps", [HC, P])
        hgt_ps = ps("hgt_ps", [H])
        l3_ps = ps("l3_ps", [H])

        s_const = sem("s_const")
        s_idx = sem("s_idx")
        s_ring = [[sem(f"s_ring_{k}{i}") for i in range(RING)] for k in ("load", "gather")]
        s_xin = sem("s_xin")
        s_xout = sem("s_xout")
        s_tr = sem("s_tr")
        s_tg = sem("s_tg")
        s_gu = sem("s_gu")
        s_d = sem("s_d")
        s_dl = sem("s_dl")
        s_silu = sem("s_silu")
        s_mul = sem("s_mul")
        s_hi = sem("s_hi")
        s_lo = sem("s_lo")
        s_mask = sem("s_mask")
        s_x1 = sem("s_x1")
        s_w = sem("s_w")
        s_w13 = sem("s_w13")
        s_x1in = [sem(f"s_x1in{i}") for i in range(2)]
        s_whi = sem("s_whi")
        s_wlo = sem("s_wlo")
        s_lang = sem("s_lang")
        s_bd = sem("s_bd")
        s_bdhi = sem("s_bdhi")
        s_bdlo = sem("s_bdlo")
        s_x1hi = sem("s_x1hi")
        s_x1lo = sem("s_x1lo")
        s_l1 = sem("s_l1")
        s_x2 = sem("s_x2")
        s_x2t = sem("s_x2t")
        s_x2thi = sem("s_x2thi")
        s_x2tlo = sem("s_x2tlo")
        s_base = sem("s_base")
        s_dve = sem("s_dve")
        s_gap = sem("s_gap")
        s_exp = sem("s_exp")
        s_hg = sem("s_hg")
        s_hgt = sem("s_hgt")
        s_hgthi = sem("s_hgthi")
        s_hgtlo = sem("s_hgtlo")
        s_l2 = sem("s_l2")
        s_x3 = sem("s_x3")
        s_x3hi = sem("s_x3hi")
        s_x3lo = sem("s_x3lo")
        s_l3 = sem("s_l3")
        s_y = sem("s_y")
        s_out = [sem(f"s_out{i}") for i in range(2)]

        def slot(it):
            return ring[:, item_no[it] % RING, :]

        def slot_width(it):
            kind = it[0]
            if kind == "wgu":
                return HC * cw(it[1])
            if kind == "b":
                return QUADS * 2 * cw(it[1] % FC)
            if kind == "ad":
                a, b = AD_PIECES[it[2]]
                return min(b * P, F) - a * P
            return H

        def wgu_at(c, m, part):
            w = cw(c)
            at = c * 4 * H + (part * 2 + m) * HC * w
            return wgu_sb[:, at:at + HC * w]

        def landing(it):
            return s_ring[it[0] in GATHERED][item_no[it] % RING]

        def wait_item(eng, it):
            eng.wait_ge(landing(it), arrived[it])

        def wait_slot_free(eng, it):
            n = item_no[it] - RING
            if n >= 0:
                before = items[n]
                if before in tr_no:
                    eng.wait_ge(s_tr, tr_no[before])
                else:
                    eng.wait_ge(s_lo, pair_no[before])

        def outputs_of(job):
            kind = job[0]
            raw = slot(job)[:, 0:slot_width(job)]
            if kind == "wgu":
                _, c, m = job
                return raw, wgu_at(c, m, 0), wgu_at(c, m, 1)
            if kind == "wd":
                c = job[1]
                k = cw(c)
                return raw[0:k], wd_sb[0:k, c, 0, :], wd_sb[0:k, c, 1, :]
            if kind == "x":
                _, g, h = job
                hc = slice(h * HC // 2, (h + 1) * HC // 2)
                return (raw.rearrange("p (c n) -> p c n", n=GROUP), xt[:, g % 2, hc, 0, :], xt[:, g % 2, hc, 1, :])
            if kind == "bd":
                _, g, q = job
                return raw, bd_hl[:, q, 0, :], bd_hl[:, q, 1, :]
            raise ValueError(kind)

        s_lo_of = lambda job: pair_no[job]

        block = ctx.enter_context(nc.Block())

        @block.sync
        def _(sp):
            sp.dma_start(itok[:, 0, :], it_lora.partition_broadcast(P)).then_inc(s_const, 16)
            sp.dma_start(const_sb[:], consts).then_inc(s_const, 16)
            sp.dma_start(itok[:, 1, :], it_cond.partition_broadcast(P)).then_inc(s_const, 16)
            sp.dma_start(itok[:, 2, :], it_lang.partition_broadcast(P)).then_inc(s_const, 16)

            def store_group(g):
                sp.wait_ge(s_x1, QUADS * (g + 1))
                sp.dma_start(x_scratch[g * GROUP:(g + 1) * GROUP, :].rearrange("(q p) h -> p q h", p=P),
                             x_res[:]).then_inc(s_xout, 16)

            for s in range(-1, STEPS):
                g, f = divmod(s, FC)
                if f == 2 and g > 0:
                    store_group(g - 1)
                if f == 4:
                    sp.wait_ge(s_xout, 16 * g)
                    sp.dma_start(x_res[:], x_rows[g * GROUP:(g + 1) * GROUP, :]
                                 .rearrange("(q p) h -> p q h", p=P)).then_inc(s_xin, 16)
                for it in staged_items(s):
                    kind = it[0]
                    if kind in GATHERED:
                        continue
                    wait_slot_free(sp, it)
                    dst = slot(it)[:, 0:slot_width(it)]
                    if kind == "wgu":
                        _, c, m = it
                        at = c * 2 * H + m * HC * cw(c)
                        src = wgu[:, at:at + HC * cw(c)]
                    elif kind == "wd":
                        c = it[1]
                        dst = dst[0:cw(c)]
                        src = wd[c * P:c * P + cw(c), :]
                    else:
                        _, gg, h = it
                        src = x_t[:, gg, h * H:(h + 1) * H]
                    sp.dma_start(dst, src).then_inc(landing(it), 16)
            sp.wait_ge(s_gu, STEPS - 4)
            sp.dma_start(w_raw[:, 0:HC * H].rearrange("p (c o) -> p c o", c=HC),
                         w2_t.rearrange("(c p) o -> p c o", p=P)).then_inc(s_w, 16)
            sp.dma_start(w_raw[:, HC * H:HC * H + HC * RA], ra_t).then_inc(s_w, 16)
            sp.dma_start(w_raw[:, HC * (H + RA):], b2).then_inc(s_w, 16)

            def load_tile(t):
                if t >= 2:
                    sp.wait_ge(s_x2, t - 1)
                sp.dma_start(x1[:, t % 2, :], x_scratch[t * P:(t + 1) * P, :]).then_inc(s_x1in[t % 2], 16)

            load_tile(0)
            load_tile(1)
            store_group(NG - 1)
            sp.wait_ge(s_xout, 16 * NG)
            for t in range(2, NT + 5):
                if t < NT:
                    load_tile(t)
                if t >= 5:
                    u = t - 5
                    sp.wait_ge(s_y, u + 1)
                    sp.dma_start(out[u * P:(u + 1) * P, :], y[:, u % 2, :]).then_inc(s_out[u % 2], 16)
            for i in range(2):
                sp.wait_ge(s_out[i], 16 * (NT // 2))

        @block.gpsimd
        def _(pool):
            def gather(dst, table, idx, s):
                nc.gpsimd.indirect_dma_start(
                    out=dst, out_offset=None, in_=table,
                    in_offset=bass.IndirectOffsetOnAxis(ap=idx, axis=0)).then_inc(s, 16)

            pool.wait_ge(s_idx, N_IDX)
            for s in range(-1, STEPS):
                for it in staged_items(s):
                    kind = it[0]
                    if kind not in GATHERED:
                        continue
                    wait_slot_free(pool, it)
                    landed = landing(it)
                    if kind == "b":
                        gg, c = divmod(it[1], FC)
                        for q in range(QUADS):
                            quad = gg * QUADS + q
                            gather(slot(it)[:, q * 2 * cw(c):(q + 1) * 2 * cw(c)], b_gu[c],
                                   idx_dup[:, quad:quad + 1], landed)
                    elif kind == "bd":
                        quad = it[1] * QUADS + it[2]
                        gather(slot(it), b_d, idx_dup[:, quad:quad + 1], landed)
                    elif kind == "agu":
                        quad = it[1] * QUADS + it[2]
                        gather(slot(it), a_gu, idx_gu[:, quad:quad + 1], landed)
                    else:
                        gather(slot(it)[:, 0:slot_width(it)], a_d[it[2]], idx_oct[:, it[1]:it[1] + 1], landed)
            pool.wait_ge(s_gu, STEPS - 4)
            for t in range(NT):
                gather(w13_raw[:, t, :], w13, idx_tok[:, t:t + 1], s_w13)
            pool.wait_ge(s_w13, 16 * NT)

            def block_diagonals(t):
                if t >= 2:
                    pool.wait_ge(s_bdlo, t - 1)
                if t == 0:
                    pool.wait_ge(s_dl, NG)
                for m in range(2):
                    ins = pool.tensor_tensor(
                        bd_raw[:, t % 2, m, :].rearrange("p (b d) -> p b d", b=QB),
                        w13_raw[:, t, m * CH:(m + 1) * CH].unsqueeze(1).to_broadcast([P, QB, CH]),
                        const("is_tok").unsqueeze(2).to_broadcast([P, QB, CH]), ALU.mult)
                ins.then_inc(s_bd, 1)

            def lows(t):
                pool.wait_ge(s_bdhi, t + 1)
                pool.tensor_tensor(bd13_hl[:, t % BD, 1, :, :], bd_raw[:, t % 2, :, :],
                                   bd13_hl[:, t % BD, 0, :, :].bitcast(F32), ALU.subtract).then_inc(s_bdlo, 1)
                pool.wait_ge(s_x1hi, t + 1)
                pool.tensor_tensor(x1_hl[:, t % 2, 1, :], x1[:, t % 2, :],
                                   x1_hl[:, t % 2, 0, :].bitcast(F32), ALU.subtract).then_inc(s_x1lo, 1)

            def low_x3(t):
                pool.wait_ge(s_x3hi, t + 1)
                pool.tensor_tensor(x3_hl[:, t % 2, 1, :], x3[:, t % 3, :],
                                   x3_hl[:, t % 2, 0, :].bitcast(F32), ALU.subtract).then_inc(s_x3lo, 1)

            block_diagonals(0)
            lows(0)
            block_diagonals(1)
            lows(1)
            for i in range(NT + 2):
                if i + 2 < NT:
                    block_diagonals(i + 2)
                if 0 <= i - 2:
                    low_x3(i - 2)
                if i + 2 < NT:
                    lows(i + 2)

        @block.scalar
        def _(sc):
            def hi(out_, in_, last=True):
                ins = sc.copy(out_, in_)
                if last:
                    ins.then_inc(s_hi, 1)

            def job_hi(job):
                kind = job[0]
                if kind == "x1":
                    return
                if kind == "act":
                    s = job[1]
                    f = s % FC
                    k = cw(f)
                    sc.wait_ge(s_gu, s + 1)
                    if s >= 2:
                        sc.wait_ge(s_lo, s_lo_of(("act", s - 2)))
                    sc.activation(act[0:k, s % 2, :], gu_ps[s % 2][0:k, 0, :], ACT.Silu).then_inc(s_silu, 1)
                    sc.wait_ge(s_mul, s + 1)
                    if s >= 2:
                        sc.wait_ge(s_d, s - 1)
                    hi(act_hl[0:k, s % 2, 0, :], act[0:k, s % 2, :])
                elif kind == "at":
                    _, g, q = job
                    sc.wait_ge(s_tr, tr_no[("agu", g, q)])
                    if g * QUADS + q > 0:
                        sc.wait_ge(s_tg, g * QUADS + q)
                    hi(agu_t[:, 0, :, :], tr_gu_ps[:])
                elif kind == "adt":
                    _, g, n = job
                    a, b = AD_PIECES[n]
                    sc.wait_ge(s_tr, tr_no[("ad", g, n)])
                    for c0, c1 in spans(a, b):
                        k = cw(c0)
                        hi(ad_t[0:k, c0:c1, :, 0, :],
                           tr_d_ps[0:k, c0 - a:c1 - a, :].rearrange("p c (q r) -> p c q r", q=QUADS), c1 == b)
                elif kind == "t":
                    g = job[1]
                    sc.wait_ge(s_mask, mask_no(("t", g)))
                    if g >= 2:
                        sc.wait_ge(s_gu, (g - 1) * FC)
                    for m in range(2):
                        for half in range(2):
                            hi(t_hl[half * HALF:(half + 1) * HALF, g % 2, m, 0, :],
                               t_raw[m * HALF:(m + 1) * HALF, :], (m, half) == (1, 1))
                elif kind == "td":
                    g = job[1]
                    sc.wait_ge(s_mask, mask_no(("td", g)))
                    if g >= 1:
                        sc.wait_ge(s_dl, g)
                    hi(td_hl[:, 0, :], td_raw[:])
                elif kind == "b":
                    s = job[1]
                    w = slot_width(job)
                    wait_item(sc, job)
                    if s >= 2:
                        sc.wait_ge(s_gu, s - 1)
                    hi(b_sel[:, s % 2, 0:w], slot(job)[:, 0:w])
                else:
                    wait_item(sc, job)
                    if kind == "x" and job[1] >= 2:
                        sc.wait_ge(s_gu, (job[1] - 1) * FC)
                    if kind == "bd" and job[1] >= 1:
                        sc.wait_ge(s_dl, job[1])
                    raw, h, _ = outputs_of(job)
                    hi(h, raw)

            for s in range(-1, STEPS + 2):
                for job in lane_jobs(s):
                    job_hi(job)
                if s == STEPS - 1:
                    sc.wait_ge(s_w, 48)
                    sc.copy(w2_hl[:, 0, :, :], w_raw[:, 0:HC * H].rearrange("p (c o) -> p c o", c=HC))
                    sc.copy(ra_hl[:, 0, :, :], w_raw[:, HC * H:HC * (H + RA)].rearrange("p (c o) -> p c o", c=HC))
                    sc.copy(b2_hl[:, 0, :], w_raw[:, HC * (H + RA):]).then_inc(s_whi, 1)

            sc.wait_ge(s_dl, NG)
            def highs(t):
                sc.wait_ge(s_bd, t + 1)
                if t >= BD:
                    sc.wait_ge(s_l3, t - BD + 1)
                sc.copy(bd13_hl[:, t % BD, 0, :, :], bd_raw[:, t % 2, :, :]).then_inc(s_bdhi, 1)
                sc.wait_ge(s_x1in[t % 2], 16 * (t // 2 + 1))
                if t >= 2:
                    sc.wait_ge(s_l1, t - 1)
                sc.copy(x1_hl[:, t % 2, 0, :], x1[:, t % 2, :]).then_inc(s_x1hi, 1)

            def high_x2t(t):
                sc.wait_ge(s_x2t, t + 1)
                if t >= 2:
                    sc.wait_ge(s_base, t - 1)
                sc.copy(x2t_hl[:, t % 2, 0, :, :], x2t_ps[:]).then_inc(s_x2thi, 1)

            highs(0)
            highs(1)
            high_x2t(0)
            for i in range(NT + 2):
                if 0 <= i - 2:
                    t = i - 2
                    sc.wait_ge(s_x3, t + 1)
                    if t >= 2:
                        sc.wait_ge(s_l3, t - 1)
                    sc.copy(x3_hl[:, t % 2, 0, :], x3[:, t % 3, :]).then_inc(s_x3hi, 1)
                if i + 2 < NT:
                    highs(i + 2)
                if 0 <= i - 1 < NT:
                    t = i - 1
                    sc.wait_ge(s_gap, t + 1)
                    sc.activation(route[:, t % 2, 17:18], route[:, t % 2, 16:17], ACT.Exp,
                                  scale=-1.0).then_inc(s_exp, 1)
                if i + 1 < NT:
                    high_x2t(i + 1)
                if 0 <= i - 1 < NT:
                    t = i - 1
                    sc.wait_ge(s_hgt, t + 1)
                    if t >= 2:
                        sc.wait_ge(s_l2, t - 1)
                    sc.copy(hgt_hl[:, t % 2, 0, :], hgt_ps[:, 0:P]).then_inc(s_hgthi, 1)

        @block.vector
        def _(ve):
            sub = [0]

            def step(ins):
                sub[0] += 1
                ins.then_inc(s_idx, 1)
                ve.wait_ge(s_idx, sub[0])

            ve.wait_ge(s_const, 64)
            for n, (v, mask, k, idx, row, mul) in enumerate((
                    (0, "is_quad", QB, None, None, 0), (0, "is_oct", 2 * QB, idx_oct, "row_rank", RANK),
                    (1, "is_tok", QB, idx_tok, "row_ch", CH), (2, "is_tok", QB, None, None, 0))):
                t = BATCHES // k
                step(ve.tensor_tensor(picked[:].rearrange("p (t k) -> p t k", k=k),
                                      itok[:, v, :].rearrange("p (t k) -> p t k", k=k),
                                      const(mask).unsqueeze(1).to_broadcast([P, t, k]), ALU.mult))
                step(ve.tensor_reduce(sel[:, n, 0:t], picked[:].rearrange("p (t k) -> p t k", k=k), AX_X, ALU.add))
                if idx is not None:
                    step(ve.tensor_scalar(idx[:], sel[:, n, 0:t], float(mul), const(row), ALU.mult, ALU.add))
            step(ve.tensor_scalar(idx_gu[:], sel[:, 0, :], float(RANK), const("row_gu"), ALU.mult, ALU.add))
            step(ve.tensor_scalar(idx_dup[:], sel[:, 0, :], float(RANK), const("row_rank"), ALU.mult, ALU.add))
            assert sub[0] == N_IDX

            def lo(out_, raw, high, last=True):
                ins = ve.tensor_tensor(out_, raw, high.bitcast(F32), ALU.subtract)
                if last:
                    ins.then_inc(s_lo, 1)

            def job_lo(job):
                kind = job[0]
                if kind == "x1":
                    g = job[1]
                    ve.wait_ge(s_xin, 16 * (g + 1))
                    ve.wait_ge(s_dl, g + 1)
                    for q in range(QUADS):
                        ve.tensor_tensor(x_res[:, q, :], x_res[:, q, :], down_ps[q][:], ALU.add).then_inc(s_x1, 1)
                    return
                if kind == "act":
                    s = job[1]
                    k = cw(s % FC)
                    ve.wait_ge(s_silu, s + 1)
                    ve.tensor_tensor(act[0:k, s % 2, :], act[0:k, s % 2, :], gu_ps[s % 2][0:k, 1, :],
                                     ALU.mult).then_inc(s_mul, 1)
                    ve.wait_ge(s_hi, pair_no[job])
                    lo(act_hl[0:k, s % 2, 1, :], act[0:k, s % 2, :], act_hl[0:k, s % 2, 0, :])
                elif kind == "at":
                    ve.wait_ge(s_hi, pair_no[job])
                    lo(agu_t[:, 1, :, :], tr_gu_ps[:], agu_t[:, 0, :, :])
                elif kind == "adt":
                    a, b = AD_PIECES[job[2]]
                    ve.wait_ge(s_hi, pair_no[job])
                    for c0, c1 in spans(a, b):
                        k = cw(c0)
                        lo(ad_t[0:k, c0:c1, :, 1, :],
                           tr_d_ps[0:k, c0 - a:c1 - a, :].rearrange("p c (q r) -> p c q r", q=QUADS),
                           ad_t[0:k, c0:c1, :, 0, :], c1 == b)
                elif kind == "t":
                    g = job[1]
                    ve.wait_ge(s_tg, QUADS * (g + 1))
                    masked(t_raw, tg_ps)
                    ve.wait_ge(s_hi, pair_no[job])
                    for m in range(2):
                        raw = t_raw[m * HALF:(m + 1) * HALF, :]
                        for half in range(2):
                            lo(t_hl[half * HALF:(half + 1) * HALF, g % 2, m, 1, :], raw,
                               t_hl[m * HALF:(m + 1) * HALF, g % 2, m, 0, :], (m, half) == (1, 1))
                elif kind == "td":
                    g = job[1]
                    ve.wait_ge(s_d, FC * (g + 1))
                    masked(td_raw, td_ps)
                    ve.wait_ge(s_hi, pair_no[job])
                    lo(td_hl[:, 1, :], td_raw[:], td_hl[:, 0, :])
                elif kind == "b":
                    s = job[1]
                    w = slot_width(job)
                    ve.wait_ge(s_hi, pair_no[job])
                    lo(b_sel[HALF:P, s % 2, 0:w], slot(job)[HALF:P, 0:w], b_sel[HALF:P, s % 2, 0:w])
                else:
                    ve.wait_ge(s_hi, pair_no[job])
                    raw, h, l = outputs_of(job)
                    lo(l, raw, h)

            def masked(dst, src_ps):
                ve.tensor_tensor(dst[:].rearrange("p (q n) -> p q n", q=QUADS),
                                 src_ps[:, 0, :].rearrange("p (q n) -> p q n", q=QUADS),
                                 const("mask").unsqueeze(1).to_broadcast([P, QUADS, P]), ALU.mult).then_inc(s_mask, 1)

            for s in range(-1, STEPS + 2):
                for job in lane_jobs(s):
                    job_lo(job)
                if s == STEPS - 1:
                    ve.wait_ge(s_whi, 1)
                    lo_w = lambda l, raw, h: ve.tensor_tensor(l, raw, h.bitcast(F32), ALU.subtract)
                    lo_w(w2_hl[:, 1, :, :], w_raw[:, 0:HC * H].rearrange("p (c o) -> p c o", c=HC), w2_hl[:, 0, :, :])
                    lo_w(ra_hl[:, 1, :, :], w_raw[:, HC * H:HC * (H + RA)].rearrange("p (c o) -> p c o", c=HC),
                         ra_hl[:, 0, :, :])
                    lo_w(b2_hl[:, 1, :], w_raw[:, HC * (H + RA):], b2_hl[:, 0, :]).then_inc(s_wlo, 1)
                    ve.tensor_tensor(lang5[:], const("iota").unsqueeze(1).to_broadcast([P, NT, EXPERTS]),
                                     sel[:, 3, :].unsqueeze(2).to_broadcast([P, NT, EXPERTS]),
                                     ALU.is_equal).then_inc(s_lang, 1)
                    ve.wait_ge(s_lang, 1)
                    ve.tensor_scalar(lang5[:], lang5[:], LANG_BIAS, None, ALU.mult).then_inc(s_lang, 1)

            chain = [0]

            def link(ins):
                chain[0] += 1
                ins.then_inc(s_dve, 1)
                ve.wait_ge(s_dve, chain[0])

            def add_x2(t):
                ve.wait_ge(s_l1, t + 1)
                if t >= 3:
                    ve.wait_ge(s_x3, t - 2)
                ve.tensor_tensor(x2[:, t % 3, :], x1[:, t % 2, :], l1_ps[:], ALU.add).then_inc(s_x2, 1)

            def low_x2t(t):
                ve.wait_ge(s_x2thi, t + 1)
                ve.tensor_tensor(x2t_hl[:, t % 2, 1, :, :], x2t_ps[:], x2t_hl[:, t % 2, 0, :, :].bitcast(F32),
                                 ALU.subtract).then_inc(s_x2tlo, 1)

            def routing(t):
                r = route[:, t % 2, :]
                logits, top, gap, e, e1, w0, w1, ids, g0, g1 = (
                    r[:, 0:8], r[:, 8:16], r[:, 16:17], r[:, 17:18], r[:, 18:19], r[:, 19:20], r[:, 20:21],
                    r[:, 24:32], r[:, 32:40], r[:, 40:48])
                ve.wait_ge(s_base, t + 1)
                if t == 0:
                    ve.wait_ge(s_lang, 2)
                link(ve.tensor_tensor(logits, ra_ps[t % 2][:, 0:EXPERTS], lang5[:, t, :], ALU.add))
                link(ve.max(top, logits))
                ve.tensor_tensor(gap, top[:, 0:1], top[:, 1:2], ALU.subtract).then_inc(s_gap, 1)
                link(ve.max_index(order[:, t % 2, :], top, logits))
                link(ve.tensor_copy(ids, order[:, t % 2, :]))
                ve.wait_ge(s_exp, t + 1)
                link(ve.tensor_scalar(e1, e, 1.0, None, ALU.add))
                link(ve.reciprocal(w0, e1))
                ve.tensor_scalar(w0, w0, SCALING, None, ALU.mult).then_inc(s_dve, 1)
                chain[0] += 1
                ve.wait_ge(s_dve, chain[0])
                link(ve.tensor_tensor(w1, w0, e, ALU.mult))
                link(ve.tensor_scalar(g0, const("iota"), ids[:, 0:1], w0, ALU.is_equal, ALU.mult))
                link(ve.tensor_scalar(g1, const("iota"), ids[:, 1:2], w1, ALU.is_equal, ALU.mult))
                link(ve.tensor_tensor(g0, g0, g1, ALU.add))
                if t >= 2:
                    ve.wait_ge(s_hgt, t - 1)
                ve.tensor_tensor(hg[:, t % 2, :].rearrange("p (e r) -> p e r", r=RANK),
                                 ra_ps[t % 2][:, EXPERTS:RA].rearrange("p (e r) -> p e r", r=RANK),
                                 g0.unsqueeze(2).to_broadcast([P, EXPERTS, RANK]), ALU.mult).then_inc(s_hg, 1)

            add_x2(0)
            low_x2t(0)
            for i in range(NT + 2):
                if 0 <= i - 2:
                    t = i - 2
                    ve.wait_ge(s_l2, t + 1)
                    if t >= 3:
                        ve.wait_ge(s_y, t - 2)
                    ve.tensor_tensor(x3[:, t % 3, :], x2[:, t % 3, :], base_ps[t % 2][:], ALU.add).then_inc(s_x3, 1)
                if i + 1 < NT:
                    add_x2(i + 1)
                if 0 <= i - 1 < NT:
                    routing(i - 1)
                if i + 1 < NT:
                    low_x2t(i + 1)
                if 0 <= i - 1 < NT:
                    t = i - 1
                    ve.wait_ge(s_hgthi, t + 1)
                    ve.tensor_tensor(hgt_hl[:, t % 2, 1, :], hgt_ps[:, 0:P], hgt_hl[:, t % 2, 0, :].bitcast(F32),
                                     ALU.subtract).then_inc(s_hgtlo, 1)
                if 0 <= i - 2:
                    t = i - 2
                    ve.wait_ge(s_l3, t + 1)
                    if t >= 2:
                        ve.wait_ge(s_out[t % 2], 16 * (t // 2))
                    ve.tensor_tensor(y[:, t % 2, :], x3[:, t % 3, :], l3_ps[:], ALU.add).then_inc(s_y, 1)

        @block.tensor
        def _(pe):
            def product(out_, stationary, moving, start, stop):
                pe.matmul(out_, stationary[0], moving[0], start=start, stop=False, skip_group_check=True)
                pe.matmul(out_, stationary[0], moving[1], start=False, stop=False, skip_group_check=True)
                return pe.matmul(out_, stationary[1], moving[0], start=False, stop=stop, skip_group_check=True)

            def transpose_agu(g, q):
                it = ("agu", g, q)
                wait_item(pe, it)
                if (g, q) == (0, 0):
                    pe.wait_ge(s_const, 64)
                else:
                    before = (g, q - 1) if q else (g - 1, QUADS - 1)
                    pe.wait_ge(s_lo, s_lo_of(("at",) + before))
                for c in range(HC):
                    mm = pe.transpose(tr_gu_ps[:, c, :], slot(it)[:, c * P:(c + 1) * P], ident)
                mm.then_inc(s_tr, 1)

            def transpose_ad(g, n):
                it = ("ad", g, n)
                a, b = AD_PIECES[n]
                wait_item(pe, it)
                if (g, n) != (0, 0):
                    before = (g, n - 1) if n else (g - 1, len(AD_PIECES) - 1)
                    pe.wait_ge(s_lo, s_lo_of(("adt",) + before))
                for c in range(a, b):
                    at = (c - a) * P
                    mm = pe.transpose(tr_d_ps[0:cw(c), c - a, :], slot(it)[:, at:at + cw(c)], ident)
                mm.then_inc(s_tr, 1)

            def x_a(g, q):
                if q == 0:
                    pe.wait_ge(s_lo, s_lo_of(("x", g, 1)))
                pe.wait_ge(s_lo, s_lo_of(("at", g, q)))
                if q == 0 and g >= 1:
                    pe.wait_ge(s_lo, s_lo_of(("t", g - 1)))
                rows = slice(q * P, (q + 1) * P)
                for c in range(HC):
                    mm = product(tg_ps[:, 0, rows], (agu_t[:, 0, c, :], agu_t[:, 1, c, :]),
                                 (xt[:, g % 2, c, 0, rows], xt[:, g % 2, c, 1, rows]), c == 0, c == HC - 1)
                mm.then_inc(s_tg, 1)

            def gate_up_base(s):
                g, f = divmod(s, FC)
                w = cw(f)
                if s >= 2:
                    pe.wait_ge(s_mul, s - 1)
                if f == 0:
                    pe.wait_ge(s_lo, s_lo_of(("x", g, 1)))
                for m in range(2):
                    if g == 0:
                        pe.wait_ge(s_lo, s_lo_of(("wgu", f, m)))
                    for c in range(HC):
                        cols = slice(c * w, (c + 1) * w)
                        product(gu_ps[s % 2][0:w, m, :], (wgu_at(f, m, 0)[:, cols], wgu_at(f, m, 1)[:, cols]),
                                (xt[:, g % 2, c, 0, :], xt[:, g % 2, c, 1, :]), m == 0 and c == 0, False)

            def gate_up_adapters(s):
                g, f = divmod(s, FC)
                w = cw(f)
                pe.wait_ge(s_lo, s_lo_of(("b", s)))
                if f == 0:
                    pe.wait_ge(s_lo, s_lo_of(("t", g)))
                for m in range(2):
                    for q in range(QUADS):
                        at = (q * 2 + m) * w
                        rows = slice(q * P, (q + 1) * P)
                        for part in range(2):
                            last = (m, q, part) == (1, QUADS - 1, 1)
                            mm = pe.matmul(gu_ps[s % 2][0:w, m, rows], b_sel[:, s % 2, at:at + w],
                                           t_hl[:, g % 2, m, part, rows], start=False, stop=last,
                                           skip_group_check=True)
                mm.then_inc(s_gu, 1)

            def down(s):
                g, f = divmod(s, FC)
                w = cw(f)
                pe.wait_ge(s_lo, s_lo_of(("act", s)))
                if g == 0:
                    pe.wait_ge(s_lo, s_lo_of(("wd", f)))
                for n, (a, b) in enumerate(AD_PIECES):
                    if f == a:
                        pe.wait_ge(s_lo, s_lo_of(("adt", g, n)))
                if f == 0 and g >= 1:
                    pe.wait_ge(s_x1, QUADS * g)
                    pe.wait_ge(s_mask, mask_no(("td", g - 1)))
                for q in range(QUADS):
                    rows = slice(q * P, (q + 1) * P)
                    a_hi, a_lo = act_hl[0:w, s % 2, 0, rows], act_hl[0:w, s % 2, 1, rows]
                    product(down_ps[q][:], (a_hi, a_lo), (wd_sb[0:w, f, 0, :], wd_sb[0:w, f, 1, :]), f == 0, False)
                    a_t = ad_t[0:w, f, q, :, :].rearrange("p a r -> p (a r)")
                    pe.matmul(td_ps[:, 0, rows], a_t, a_hi, start=(f == 0 and q == 0), stop=False,
                              skip_group_check=True)
                    mm = pe.matmul(td_ps[:, 0, rows], a_t, a_lo, start=False, stop=(f == FC - 1),
                                   skip_group_check=True)
                mm.then_inc(s_d, 1)

            def down_adapters(g):
                pe.wait_ge(s_lo, max(s_lo_of(("td", g)), s_lo_of(("bd", g, 1))))
                for q in range(QUADS):
                    rows = slice(q * P, (q + 1) * P)
                    mm = product(down_ps[q][:], (td_hl[:, 0, rows], td_hl[:, 1, rows]),
                                 (bd_hl[:, q, 0, :], bd_hl[:, q, 1, :]), False, True)
                mm.then_inc(s_dl, 1)

            for s in range(STEPS):
                g, f = divmod(s, FC)
                if f == 1 and g > 0:
                    down_adapters(g - 1)
                gate_up_base(s)
                if s == 0:
                    for q in range(QUADS):
                        transpose_agu(0, q)
                        x_a(0, q)
                gate_up_adapters(s)
                if s > 0:
                    down(s - 1)
                for kind, gg, n in pe_side(s):
                    {"at": transpose_agu, "tg": x_a, "adt": transpose_ad}[kind](gg, n)
            down(STEPS - 1)
            down_adapters(NG - 1)

            def mix(bank, t, m, x_hl):
                return product(bank, (bd13_hl[:, t % BD, 0, m, :], bd13_hl[:, t % BD, 1, m, :]),
                               (x_hl[:, t % 2, 0, :], x_hl[:, t % 2, 1, :]), True, True)

            def l1(t):
                pe.wait_ge(s_x1lo, t + 1)
                if t >= 1:
                    pe.wait_ge(s_x2, t)
                mix(l1_ps[:], t, 0, x1_hl).then_inc(s_l1, 1)

            def transpose_x2(t):
                pe.wait_ge(s_x2, t + 1)
                if t >= 1:
                    pe.wait_ge(s_x2tlo, t)
                for c in range(HC):
                    mm = pe.transpose(x2t_ps[:, c, :], x2[:, t % 3, c * P:(c + 1) * P], ident)
                mm.then_inc(s_x2t, 1)

            def l2_base(t, c0, c1):
                if c0 == 0:
                    pe.wait_ge(s_x2tlo, t + 1)
                    if t == 0:
                        pe.wait_ge(s_wlo, 1)
                    if t >= 2:
                        pe.wait_ge(s_x3, t - 1)
                        pe.wait_ge(s_hg, t - 1)
                for c in range(c0, c1):
                    hi_, lo_ = x2t_hl[:, t % 2, 0, c, :], x2t_hl[:, t % 2, 1, c, :]
                    b, r = base_ps[t % 2][:], ra_ps[t % 2][:, 0:RA]
                    for n, (x_part, part) in enumerate(((hi_, 0), (hi_, 1), (lo_, 0))):
                        pe.matmul(b, x_part, w2_hl[:, part, c, :], start=(c == 0 and n == 0), stop=False,
                                  skip_group_check=True)
                        mm = pe.matmul(r, x_part, ra_hl[:, part, c, :], start=(c == 0 and n == 0),
                                       stop=(c == HC - 1 and n == 2), skip_group_check=True)
                if c1 == HC:
                    mm.then_inc(s_base, 1)

            def transpose_hg(t):
                pe.wait_ge(s_hg, t + 1)
                if t >= 1:
                    pe.wait_ge(s_hgtlo, t)
                pe.transpose(hgt_ps[:, 0:P], hg[:, t % 2, :], ident).then_inc(s_hgt, 1)

            def experts(t):
                pe.wait_ge(s_hgtlo, t + 1)
                product(base_ps[t % 2][:], (hgt_hl[:, t % 2, 0, :], hgt_hl[:, t % 2, 1, :]),
                        (b2_hl[:, 0, :], b2_hl[:, 1, :]), False, True).then_inc(s_l2, 1)

            def l3(t):
                pe.wait_ge(s_x3lo, t + 1)
                if t >= 1:
                    pe.wait_ge(s_y, t)
                mix(l3_ps[:], t, 1, x3_hl).then_inc(s_l3, 1)

            pe.wait_ge(s_x1, QUADS * NG)
            l1(0)
            transpose_x2(0)
            for i in range(NT + 2):
                if i + 1 < NT:
                    l1(i + 1)
                if i < NT:
                    l2_base(i, 0, HC // 2)
                if i + 1 < NT:
                    transpose_x2(i + 1)
                if i < NT:
                    l2_base(i, HC // 2, HC)
                if 0 <= i - 1 < NT:
                    transpose_hg(i - 1)
                if 0 <= i - 2:
                    l3(i - 2)
                if 0 <= i - 1 < NT:
                    experts(i - 1)


N_IDX = 4 * 2 + 2 + 2


def spans(a, b):
    return [(a, b)] if b < FC else [(a, FC - 1), (FC - 1, FC)]


def mask_no(job):
    order = [j for s in range(-1, STEPS + FC) for j in lane_jobs(s) if j[0] in ("t", "td")]
    return order.index(job) + 1


def kernel(**inputs):
    import concourse.bacc as bacc
    from concourse.bass_utils import run_bass_kernel_spmd

    a = {k: np.asarray(v) for k, v in inputs.items()}

    def chunked_t(w, width):
        t = w.T.reshape(HC, P, -1)
        return [t[:, :, c:c + width].transpose(1, 0, 2).reshape(P, -1) for c in range(0, t.shape[2], width)]

    rows = a["x"].reshape(ROWS, H)
    wgu = [m for pair in zip(chunked_t(a["L0_cond_W_gate"], P), chunked_t(a["L0_cond_W_up"], P)) for m in pair]
    ab = ADAPTERS * RANK
    b_gate, b_up = (a[f"L0_cond_B_{k}"][0].transpose(0, 2, 1).reshape(ab, F) for k in ("gate", "up"))
    a_down = a["L0_cond_A_down"][0].reshape(ab, F)
    ra = np.concatenate([a["L2_cond_Wr"], a["L2_cond_A"].reshape(EXPERTS * RANK, H)])
    arrays = {
        "x_t": rows.T.reshape(HC, P, NG, GROUP).transpose(1, 2, 0, 3).reshape(P, NG, HC * GROUP),
        "x_rows": rows,
        "it_lora": a["itok_B_2_6"], "it_cond": a["itok_B_0_15"], "it_lang": a["itok_B_0_7"],
        "wgu": np.concatenate(wgu, axis=1),
        "wd": a["L0_cond_W_down"].T,
        "a_gu": np.concatenate([a["L0_cond_A_gate"][0].reshape(ab, H), a["L0_cond_A_up"][0].reshape(ab, H)]),
        "b_d": a["L0_cond_B_down"][0].transpose(0, 2, 1).reshape(ab, H),
        "w13": np.concatenate([a["L1_cond_weights"], a["L3_cond_weights"]], axis=2).reshape(CONDS * CH, 2 * CH),
        "w2_t": a["L2_cond_W"].T,
        "ra_t": chunked_t(ra, RA)[0],
        "b2": a["L2_cond_B"].transpose(0, 2, 1).reshape(EXPERTS * RANK, H),
        "consts": CONSTS,
    }
    for c in range(FC):
        f = slice(c * P, c * P + cw(c))
        arrays[f"b_gu{c}"] = np.concatenate([b_gate[:, f], b_up[:, f]], axis=1)
    for n, (c0, c1) in enumerate(AD_PIECES):
        arrays[f"a_d{n}"] = a_down[:, c0 * P:min(c1 * P, F)]
    arrays = {k: np.ascontiguousarray(v) for k, v in arrays.items()}

    nc = bacc.Bacc("TRN2", target_bir_lowering=False, num_devices=1)
    args = [nc.dram_tensor(k, v.shape, mybir.dt.from_np(v.dtype), kind="ExternalInput").ap()
            for k, v in arrays.items()]
    args.append(nc.dram_tensor("out", (ROWS, H), F32, kind="ExternalOutput").ap())
    bass_conditioned_residual_chain(nc, *args)
    r = run_bass_kernel_spmd(nc, [arrays], core_ids=[0])
    return r.results[0]["out"].reshape(BATCHES, CH, H)
```

```python
from contextlib import ExitStack

import numpy as np

import concourse.bass as bass
from concourse import mybir

F32 = mybir.dt.float32
F32R = mybir.dt.float32r
I32 = mybir.dt.int32
U32 = mybir.dt.uint32
ALU = mybir.AluOpType
ACT = mybir.ActivationFunctionType
AX_X = mybir.AxisListType.X

P = 128
BATCHES, CH, H = 64, 32, 512
F = 1376
RANK = 16
ADAPTERS = 16
CONDS = 16
EXPERTS = 8
LORA_SCALE = 0.5
LANG_BIAS = 5.0
SCALING = 2.0

ROWS = BATCHES * CH
HC = H // P
GROUP = 256
NG = ROWS // GROUP
GB = GROUP // CH
TILES = GROUP // P
NT = ROWS // P
TB = P // CH
FC = -(-F // P)
LASTW = F - (FC - 1) * P
STEPS = NG * FC
AD_PIECES = [(0, 4), (4, 8), (8, FC)]
PAIRS = -(-FC // 2)
GATHERED = ("b", "bd", "agu", "ad")
RING = 6
BD = 6
RA = EXPERTS + EXPERTS * RANK
L2_COLS = H + RA
L2_PART = L2_COLS // 2
BASE_AT = H - L2_PART


def cw(c):
    return P if c < FC - 1 else LASTW


CONST_COLS = {}


def const_array():
    p = np.arange(P)
    blocks = {
        "ident": np.eye(P),
        "mask": LORA_SCALE * (p[:, None] // RANK == np.arange(GROUP)[None, :] // CH),
        "is_rank": p[:, None] // RANK == np.arange(GB)[None, :],
        "is_ch": p[:, None] // CH == np.arange(TB)[None, :],
        "row_rank": (p % RANK)[:, None],
        "row_ch": (p % CH)[:, None],
        "iota": np.broadcast_to(np.arange(EXPERTS), (P, EXPERTS)),
    }
    at = 0
    for name, b in blocks.items():
        CONST_COLS[name] = (at, at + b.shape[1])
        at += b.shape[1]
    return np.concatenate([b.astype(np.float32) for b in blocks.values()], axis=1)


CONSTS = const_array()


def staged_items(s):
    g, f = divmod(s, FC)
    if s < 0:
        return [("x", 0, 0), ("wgu", 0, 0), ("x", 0, 1), ("wgu", 0, 1), ("agu", 0, 0), ("agu", 0, 1),
                ("wgu", 1, 0), ("wgu", 1, 1), ("b", 0, 0), ("wd", 0), ("ad", 0, 0)]
    out = []
    if g == 0 and f + 2 < FC:
        out += [("wgu", f + 2, 0), ("wgu", f + 2, 1)]
    if s + 2 < STEPS and (s + 2) % FC % 2 == 0:
        out.append(("b", (s + 2) // FC, (s + 2) % FC // 2))
    if g == 0 and f + 1 < FC:
        out.append(("wd", f + 1))
    if g == 0:
        out += {0: [("ad", 0, 1)], 2: [("ad", 0, 2)]}.get(f, [])
    elif f == 0:
        out.append(("ad", g, 2))
    if g + 1 < NG:
        n = g + 1
        out += {0: [("x", n, 0)], 1: [("x", n, 1), ("agu", n, 0)], 3: [("agu", n, 1)],
                4: [("ad", n, 0)], 8: [("ad", n, 1)]}.get(f, [])
    if f == 6:
        out.append(("bd", g))
    return out


def pe_side(s):
    g, f = divmod(s, FC)
    out = []
    if g == 0:
        out += {0: [("adt", 0, 0)], 1: [("adt", 0, 1)], 3: [("adt", 0, 2)]}.get(f, [])
    elif f == 0:
        out.append(("adt", g, 2))
    if g + 1 < NG:
        n = g + 1
        out += {2: [("at", n, 0)], 3: [("tg", n, 0)], 4: [("at", n, 1)], 5: [("tg", n, 1), ("adt", n, 0)],
                9: [("adt", n, 1)]}.get(f, [])
    return out


def lane_jobs(s):
    g, f = divmod(s, FC)
    if s < 0:
        jobs = [("x", 0, 0), ("wgu", 0, 0), ("x", 0, 1), ("wgu", 0, 1), ("at", 0, 0), ("wgu", 1, 0), ("at", 0, 1),
                ("wgu", 1, 1), ("t", 0), ("b", 0), ("b", 1), ("wd", 0)]
        return jobs
    jobs = []
    if f == 1 and g > 0:
        jobs.append(("x1", g - 1))
    if s < STEPS:
        jobs.append(("act", s))
    if f == 0 and g > 0:
        jobs.append(("td", g - 1))
    if s >= STEPS:
        return jobs
    jobs += [j for j in pe_side(s) if j[0] in ("adt", "at")]
    if f == 6 and g + 1 < NG:
        jobs.append(("t", g + 1))
    if s + 2 < STEPS:
        jobs.append(("b", s + 2))
    jobs += [j for j in staged_items(s) if j[0] not in ("agu", "ad", "b")]
    return jobs


def bass_conditioned_residual_chain(nc, x_t, x_rows, it_lora, it_cond, it_lang, wgu, wd, a_gate, a_up, b_d,
                                    w13, w2ra_t, b2, consts, *rest):
    b_gu, rest = rest[:PAIRS], rest[PAIRS:]
    a_d, rest = rest[:len(AD_PIECES)], rest[len(AD_PIECES):]
    (out,) = rest

    items = [it for s in range(-1, STEPS) for it in staged_items(s)]
    item_no = {it: n for n, it in enumerate(items)}
    arrived = {}
    total = {}
    for n, it in enumerate(items):
        own = (it[0] in GATHERED, n % RING)
        total[own] = total.get(own, 0) + 16
        arrived[it] = total[own]
    pairs = [j for s in range(-1, STEPS + FC) for j in lane_jobs(s) if j[0] != "x1"]
    pair_no = {j: n + 1 for n, j in enumerate(pairs)}
    pe_read = [it for it in items if it[0] in ("agu", "ad")]
    pe_tr = [("agu", 0, 0), ("agu", 0, 1)] + [
        ({"at": "agu", "adt": "ad"}[j[0]],) + j[1:] for s in range(STEPS) for j in pe_side(s) if j[0] != "tg"]
    tr_no = {it: n + 1 for n, it in enumerate(pe_tr)}

    with ExitStack() as ctx:
        def sb(name, shape, dt=F32, stack=ctx):
            return stack.enter_context(nc.sbuf_tensor(name, [P, *shape], dt))

        def ps(name, shape, stack=ctx):
            return stack.enter_context(nc.psum_tensor(name, [P, *shape], F32))

        def sem(name):
            return ctx.enter_context(nc.semaphore(name))

        const_sb = sb("const_sb", [CONSTS.shape[1]])
        itok = sb("itok", [3, BATCHES], I32)
        picked = sb("picked", [BATCHES])
        sel = sb("sel", [3, NT])
        idx_rank = sb("idx_rank", [NG], U32)
        idx_ch = sb("idx_ch", [NT], U32)
        x_scratch = nc.dram_tensor("x_after_l0", [ROWS, H], F32, kind="Internal").ap()

        def const(name):
            a, b = CONST_COLS[name]
            return const_sb[:, a:b]

        ident = const("ident")

        mem_a = ExitStack()
        wgu_sb = sb("wgu_sb", [(FC - 1) * 4 * H + 4 * HC * LASTW], F32R, mem_a)
        wd_sb = sb("wd_sb", [FC, 2, H], F32R, mem_a)
        ring = sb("ring", [RING, H], F32, mem_a)
        xt = sb("xt", [2, HC, 2, GROUP], F32R, mem_a)
        act = sb("act", [2, GROUP], F32, mem_a)
        act_hl = sb("act_hl", [2, 2, GROUP], F32R, mem_a)
        b_sel = sb("b_sel", [2, 2, 2 * P], F32R, mem_a)
        agu_t = sb("agu_t", [2, HC, P], F32R, mem_a)
        ad_t = sb("ad_t", [FC, 2, P], F32R, mem_a)
        t_raw = sb("t_raw", [2, GROUP], F32, mem_a)
        t_hl = sb("t_hl", [2, 2, 2, GROUP], F32R, mem_a)
        td_hl = sb("td_hl", [2, GROUP], F32R, mem_a)
        bd_hl = sb("bd_hl", [2, H], F32R, mem_a)
        x_res = sb("x_res", [TILES, H], F32, mem_a)
        mem_a.close()

        banks_a = ExitStack()
        gu_ps = [ps(f"gu_ps{i}", [2, GROUP], banks_a) for i in range(2)]
        down_ps = [ps(f"down_ps{i}", [H], banks_a) for i in range(TILES)]
        td_ps = ps("td_ps", [H], banks_a)
        tg_ps = ps("tg_ps", [2, GROUP], banks_a)
        tr_gu_ps = ps("tr_gu_ps", [HC, P], banks_a)
        tr_d_ps = ps("tr_d_ps", [4, P], banks_a)
        banks_a.close()

        w13_raw = sb("w13_raw", [NT, 2 * CH])
        x1 = sb("x1", [2, H])
        w_raw = sb("w_raw", [HC * L2_COLS + H])
        bd_raw = sb("bd_raw", [2, 2, P])
        bd13_hl = sb("bd13_hl", [BD, 2, 2, P], F32R)
        x1_hl = sb("x1_hl", [2, 2, H], F32R)
        w2ra_hl = sb("w2ra_hl", [2, HC, L2_COLS], F32R)
        b2_hl = sb("b2_hl", [2, H], F32R)
        lang5 = sb("lang5", [NT, EXPERTS])
        x2 = sb("x2", [3, H])
        x2t_hl = sb("x2t_hl", [2, 2, HC, P], F32R)
        route = sb("route", [2, 64])
        order = sb("order", [2, EXPERTS], U32)
        hg = sb("hg", [2, P])
        hgt_hl = sb("hgt_hl", [2, 2, P], F32R)
        x3 = sb("x3", [3, H])
        x3_hl = sb("x3_hl", [2, 2, H], F32R)
        y = sb("y", [2, H])

        l2_ps = [ps(f"l2_ps{i}", [2 * H]) for i in range(2)]
        hgt_ps = ps("hgt_ps", [H])
        l1_ps = ps("l1_ps", [H])
        x2t_ps = ps("x2t_ps", [HC, P])
        l3_ps = ps("l3_ps", [H])

        def base_of(t):
            return l2_ps[t % 2][:, BASE_AT:BASE_AT + H]

        def logits_of(t):
            at = BASE_AT + H
            return l2_ps[t % 2][:, at:at + EXPERTS]

        def h_of(t):
            at = BASE_AT + H + EXPERTS
            return l2_ps[t % 2][:, at:at + EXPERTS * RANK].rearrange("p (e r) -> p e r", r=RANK)

        s_const = sem("s_const")
        s_idx = sem("s_idx")
        s_ring = [[sem(f"s_ring_{k}{i}") for i in range(RING)] for k in ("load", "gather")]
        s_xin = sem("s_xin")
        s_xout = sem("s_xout")
        s_tr = sem("s_tr")
        s_tg = sem("s_tg")
        s_gu = sem("s_gu")
        s_d = sem("s_d")
        s_dl = sem("s_dl")
        s_silu = sem("s_silu")
        s_mul = sem("s_mul")
        s_hi = sem("s_hi")
        s_lo = sem("s_lo")
        s_mask = sem("s_mask")
        s_x1 = sem("s_x1")
        s_w = sem("s_w")
        s_w13 = sem("s_w13")
        s_x1in = [sem(f"s_x1in{i}") for i in range(2)]
        s_whi = sem("s_whi")
        s_wlo = sem("s_wlo")
        s_lang = sem("s_lang")
        s_bd = sem("s_bd")
        s_bdhi = sem("s_bdhi")
        s_bdlo = sem("s_bdlo")
        s_x1hi = sem("s_x1hi")
        s_x1lo = sem("s_x1lo")
        s_l1 = sem("s_l1")
        s_x2 = sem("s_x2")
        s_x2t = sem("s_x2t")
        s_x2thi = sem("s_x2thi")
        s_x2tlo = sem("s_x2tlo")
        s_base = sem("s_base")
        s_dve = sem("s_dve")
        s_gap = sem("s_gap")
        s_exp = sem("s_exp")
        s_hg = sem("s_hg")
        s_hgt = sem("s_hgt")
        s_hgthi = sem("s_hgthi")
        s_hgtlo = sem("s_hgtlo")
        s_l2 = sem("s_l2")
        s_x3 = sem("s_x3")
        s_x3hi = sem("s_x3hi")
        s_x3lo = sem("s_x3lo")
        s_l3 = sem("s_l3")
        s_y = sem("s_y")
        s_out = [sem(f"s_out{i}") for i in range(2)]

        def slot(it):
            return ring[:, item_no[it] % RING, :]

        def slot_width(it):
            kind = it[0]
            if kind == "wgu":
                return HC * cw(it[1])
            if kind == "b":
                return 2 * (min((2 * it[2] + 2) * P, F) - 2 * it[2] * P)
            if kind == "ad":
                a, b = AD_PIECES[it[2]]
                return min(b * P, F) - a * P
            return H

        def wgu_at(c, m, part):
            w = cw(c)
            at = c * 4 * H + (part * 2 + m) * HC * w
            return wgu_sb[:, at:at + HC * w]

        def landing(it):
            return s_ring[it[0] in GATHERED][item_no[it] % RING]

        def wait_item(eng, it):
            eng.wait_ge(landing(it), arrived[it])

        def wait_slot_free(eng, it):
            n = item_no[it] - RING
            if n >= 0:
                before = items[n]
                if before in tr_no:
                    eng.wait_ge(s_tr, tr_no[before])
                elif before[0] == "b":
                    _, g, pair = before
                    eng.wait_ge(s_lo, pair_no[("b", g * FC + min(2 * pair + 1, FC - 1))])
                else:
                    eng.wait_ge(s_lo, pair_no[before])

        def outputs_of(job):
            kind = job[0]
            raw = slot(job)[:, 0:slot_width(job)]
            if kind == "wgu":
                _, c, m = job
                return raw, wgu_at(c, m, 0), wgu_at(c, m, 1)
            if kind == "wd":
                c = job[1]
                k = cw(c)
                return raw[0:k], wd_sb[0:k, c, 0, :], wd_sb[0:k, c, 1, :]
            if kind == "x":
                _, g, h = job
                hc = slice(h * HC // 2, (h + 1) * HC // 2)
                return (raw.rearrange("p (c n) -> p c n", n=GROUP), xt[:, g % 2, hc, 0, :], xt[:, g % 2, hc, 1, :])
            if kind == "bd":
                return raw, bd_hl[:, 0, :], bd_hl[:, 1, :]
            raise ValueError(kind)

        def raw_b(s):
            g, f = divmod(s, FC)
            at = f % 2 * 2 * P
            return slot(("b", g, f // 2))[:, at:at + 2 * cw(f)]

        def s_lo_of(job):
            return pair_no[job]

        block = ctx.enter_context(nc.Block())

        @block.sync
        def _(sp):
            def store_group(g):
                sp.wait_ge(s_x1, TILES * (g + 1))
                sp.dma_start(x_scratch[g * GROUP:(g + 1) * GROUP, :].rearrange("(q p) h -> p q h", p=P),
                             x_res[:]).then_inc(s_xout, 16)

            for s in range(-1, STEPS):
                g, f = divmod(s, FC)
                if f == 2 and g > 0:
                    store_group(g - 1)
                if f == 4:
                    sp.wait_ge(s_xout, 16 * g)
                    sp.dma_start(x_res[:], x_rows[g * GROUP:(g + 1) * GROUP, :]
                                 .rearrange("(q p) h -> p q h", p=P)).then_inc(s_xin, 16)
                for it in staged_items(s):
                    kind = it[0]
                    if kind in GATHERED:
                        continue
                    wait_slot_free(sp, it)
                    dst = slot(it)[:, 0:slot_width(it)]
                    if kind == "wgu":
                        _, c, m = it
                        at = c * 2 * H + m * HC * cw(c)
                        src = wgu[:, at:at + HC * cw(c)]
                    elif kind == "wd":
                        c = it[1]
                        dst = dst[0:cw(c)]
                        src = wd[c * P:c * P + cw(c), :]
                    else:
                        _, gg, h = it
                        src = x_t[:, gg, h * H:(h + 1) * H]
                    sp.dma_start(dst, src).then_inc(landing(it), 16)
            def load_tile(t):
                if t >= 2:
                    sp.wait_ge(s_x2, t - 1)
                sp.dma_start(x1[:, t % 2, :], x_scratch[t * P:(t + 1) * P, :]).then_inc(s_x1in[t % 2], 16)

            sp.wait_ge(s_gu, STEPS - 7)
            load_tile(0)
            load_tile(1)
            sp.dma_start(w_raw[:, 0:HC * L2_COLS].rearrange("p (c o) -> p c o", c=HC),
                         w2ra_t.rearrange("(c p) o -> p c o", p=P)).then_inc(s_w, 16)
            sp.dma_start(w_raw[:, HC * L2_COLS:], b2).then_inc(s_w, 16)
            store_group(NG - 1)
            sp.wait_ge(s_xout, 16 * NG)
            for t in range(2, NT + 5):
                if t < NT:
                    load_tile(t)
                if t >= 5:
                    u = t - 5
                    sp.wait_ge(s_y, u + 1)
                    sp.dma_start(out[u * P:(u + 1) * P, :], y[:, u % 2, :]).then_inc(s_out[u % 2], 16)
            for i in range(2):
                sp.wait_ge(s_out[i], 16 * (NT // 2))

        @block.gpsimd
        def _(pool):
            def gather(dst, table, idx, s):
                nc.gpsimd.indirect_dma_start(
                    out=dst, out_offset=None, in_=table,
                    in_offset=bass.IndirectOffsetOnAxis(ap=idx, axis=0)).then_inc(s, 16)

            pool.wait_ge(s_idx, N_IDX)
            tables = {"bd": lambda it: b_d, "agu": lambda it: (a_gate, a_up)[it[2]],
                      "b": lambda it: b_gu[it[2]], "ad": lambda it: a_d[it[2]]}
            for s in range(-1, STEPS):
                for it in staged_items(s):
                    if it[0] in GATHERED:
                        wait_slot_free(pool, it)
                        gather(slot(it)[:, 0:slot_width(it)], tables[it[0]](it), idx_rank[:, it[1]:it[1] + 1],
                               landing(it))
                n = s - (STEPS - FC + 1)
                if n == 0:
                    pool.wait_ge(s_gu, STEPS - FC + 1)
                if n >= 0:
                    for t in range(4 * n, min(4 * n + 4, NT)):
                        gather(w13_raw[:, t, :], w13, idx_ch[:, t:t + 1], s_w13)
            pool.wait_ge(s_w13, 16 * NT)

            def block_diagonals(t):
                if t >= 2:
                    pool.wait_ge(s_bdlo, t - 1)
                if t == 0:
                    pool.wait_ge(s_gu, STEPS - 4)
                for m in range(2):
                    ins = pool.tensor_tensor(
                        bd_raw[:, t % 2, m, :].rearrange("p (b d) -> p b d", b=TB),
                        w13_raw[:, t, m * CH:(m + 1) * CH].unsqueeze(1).to_broadcast([P, TB, CH]),
                        const("is_ch").unsqueeze(2).to_broadcast([P, TB, CH]), ALU.mult)
                ins.then_inc(s_bd, 1)

            def lows(t):
                pool.wait_ge(s_bdhi, t + 1)
                pool.tensor_tensor(bd13_hl[:, t % BD, 1, :, :], bd_raw[:, t % 2, :, :],
                                   bd13_hl[:, t % BD, 0, :, :].bitcast(F32), ALU.subtract).then_inc(s_bdlo, 1)
                pool.wait_ge(s_x1hi, t + 1)
                pool.tensor_tensor(x1_hl[:, t % 2, 1, :], x1[:, t % 2, :],
                                   x1_hl[:, t % 2, 0, :].bitcast(F32), ALU.subtract).then_inc(s_x1lo, 1)

            def low_x3(t):
                pool.wait_ge(s_x3hi, t + 1)
                pool.tensor_tensor(x3_hl[:, t % 2, 1, :], x3[:, t % 3, :],
                                   x3_hl[:, t % 2, 0, :].bitcast(F32), ALU.subtract).then_inc(s_x3lo, 1)

            block_diagonals(0)
            lows(0)
            block_diagonals(1)
            lows(1)
            block_diagonals(2)
            lows(2)
            for t in range(3, NT + 4):
                if t < NT:
                    block_diagonals(t)
                if t >= 4:
                    low_x3(t - 4)
                if t < NT:
                    lows(t)

        @block.scalar
        def _(sc):
            sc.dma_start(itok[:, 0, :], it_lora.partition_broadcast(P)).then_inc(s_const, 16)
            sc.dma_start(const_sb[:], consts).then_inc(s_const, 16)
            sc.dma_start(itok[:, 1, :], it_cond.partition_broadcast(P)).then_inc(s_const, 16)
            sc.dma_start(itok[:, 2, :], it_lang.partition_broadcast(P)).then_inc(s_const, 16)

            def hi(out_, in_, last=True):
                ins = sc.copy(out_, in_)
                if last:
                    ins.then_inc(s_hi, 1)

            def job_hi(job):
                kind = job[0]
                if kind == "x1":
                    return
                if kind == "act":
                    s = job[1]
                    f = s % FC
                    k = cw(f)
                    sc.wait_ge(s_gu, s + 1)
                    if s >= 2:
                        sc.wait_ge(s_lo, s_lo_of(("act", s - 2)))
                    sc.activation(act[0:k, s % 2, :], gu_ps[s % 2][0:k, 0, :], ACT.Silu).then_inc(s_silu, 1)
                    sc.wait_ge(s_mul, s + 1)
                    if s >= 2:
                        sc.wait_ge(s_d, s - 1)
                    hi(act_hl[0:k, s % 2, 0, :], act[0:k, s % 2, :])
                elif kind == "at":
                    _, g, m = job
                    sc.wait_ge(s_tr, tr_no[("agu", g, m)])
                    if 2 * g + m > 0:
                        sc.wait_ge(s_tg, 2 * g + m)
                    hi(agu_t[:, 0, :, :], tr_gu_ps[:])
                elif kind == "adt":
                    _, g, n = job
                    a, b = AD_PIECES[n]
                    sc.wait_ge(s_tr, tr_no[("ad", g, n)])
                    for c0, c1 in spans(a, b):
                        k = cw(c0)
                        hi(ad_t[0:k, c0:c1, 0, :], tr_d_ps[0:k, c0 - a:c1 - a, :], c1 == b)
                elif kind == "t":
                    g = job[1]
                    sc.wait_ge(s_mask, mask_no(("t", g)))
                    if g >= 2:
                        sc.wait_ge(s_gu, (g - 1) * FC)
                    hi(t_hl[:, g % 2, 0, :, :], t_raw[:])
                elif kind == "td":
                    g = job[1]
                    sc.wait_ge(s_mask, mask_no(("td", g)))
                    if g >= 1:
                        sc.wait_ge(s_dl, g)
                    hi(td_hl[:, 0, :], t_raw[:, 0, :])
                elif kind == "b":
                    s = job[1]
                    wait_item(sc, ("b", s // FC, s % FC // 2))
                    if s >= 2:
                        sc.wait_ge(s_gu, s - 1)
                    hi(b_sel[:, s % 2, 0, 0:2 * cw(s % FC)], raw_b(s))
                else:
                    wait_item(sc, job)
                    if kind == "x" and job[1] >= 2:
                        sc.wait_ge(s_gu, (job[1] - 1) * FC)
                    if kind == "bd" and job[1] >= 1:
                        sc.wait_ge(s_dl, job[1])
                    raw, h, _ = outputs_of(job)
                    hi(h, raw)

            def high_x2t(t):
                sc.wait_ge(s_x2t, t + 1)
                if t >= 2:
                    sc.wait_ge(s_base, t - 1)
                sc.copy(x2t_hl[:, t % 2, 0, :, :], x2t_ps[:]).then_inc(s_x2thi, 1)

            def high_hgt(t):
                sc.wait_ge(s_hgt, t + 1)
                if t >= 2:
                    sc.wait_ge(s_l2, t - 1)
                sc.copy(hgt_hl[:, t % 2, 0, :], hgt_ps[:, 0:P]).then_inc(s_hgthi, 1)

            def high_x3(t):
                sc.wait_ge(s_x3, t + 1)
                if t >= 2:
                    sc.wait_ge(s_l3, t - 1)
                sc.copy(x3_hl[:, t % 2, 0, :], x3[:, t % 3, :]).then_inc(s_x3hi, 1)

            def exponential(t):
                sc.wait_ge(s_gap, t + 1)
                sc.activation(route[:, t % 2, 17:18], route[:, t % 2, 16:17], ACT.Exp, scale=-1.0).then_inc(s_exp, 1)

            def highs(t):
                sc.wait_ge(s_bd, t + 1)
                if t >= BD:
                    sc.wait_ge(s_l3, t - BD + 1)
                sc.copy(bd13_hl[:, t % BD, 0, :, :], bd_raw[:, t % 2, :, :]).then_inc(s_bdhi, 1)
                sc.wait_ge(s_x1in[t % 2], 16 * (t // 2 + 1))
                if t >= 2:
                    sc.wait_ge(s_l1, t - 1)
                sc.copy(x1_hl[:, t % 2, 0, :], x1[:, t % 2, :]).then_inc(s_x1hi, 1)

            for s in range(-1, STEPS + 2):
                for job in lane_jobs(s):
                    job_hi(job)
                if s == STEPS - 2:
                    sc.wait_ge(s_w, 32)
                    sc.copy(w2ra_hl[:, 0, :, :], w_raw[:, 0:HC * L2_COLS].rearrange("p (c o) -> p c o", c=HC))
                    sc.copy(b2_hl[:, 0, :], w_raw[:, HC * L2_COLS:]).then_inc(s_whi, 1)
                if s == STEPS - 3:
                    highs(0)
                    highs(1)
                if s == STEPS - 1:
                    high_x2t(0)
            for i in range(NT + 1):
                if i >= 1:
                    high_hgt(i - 1)
                if i + 1 < NT:
                    high_x2t(i + 1)
                if i < NT:
                    exponential(i)
                if i >= 1:
                    high_x3(i - 1)
                if i == 0:
                    highs(2)
                if i + 3 < NT:
                    highs(i + 3)

        @block.vector
        def _(ve):
            sub = [0]

            def step(ins):
                sub[0] += 1
                ins.then_inc(s_idx, 1)
                ve.wait_ge(s_idx, sub[0])

            ve.wait_ge(s_const, 64)
            for n, (v, mask, k, idx, row) in enumerate((
                    (0, "is_rank", GB, idx_rank, "row_rank"), (1, "is_ch", TB, idx_ch, "row_ch"),
                    (2, "is_ch", TB, None, None))):
                t = BATCHES // k
                by_batch = dict(k=k)
                step(ve.tensor_tensor(picked[:].rearrange("p (t k) -> p t k", **by_batch),
                                      itok[:, v, :].rearrange("p (t k) -> p t k", **by_batch),
                                      const(mask).unsqueeze(1).to_broadcast([P, t, k]), ALU.mult))
                step(ve.tensor_reduce(sel[:, n, 0:t], picked[:].rearrange("p (t k) -> p t k", **by_batch),
                                      AX_X, ALU.add))
                if idx is not None:
                    step(ve.tensor_scalar(idx[:], sel[:, n, 0:t], float(P // k), const(row), ALU.mult, ALU.add))
            assert sub[0] == N_IDX

            def lo(out_, raw, high, last=True):
                ins = ve.tensor_tensor(out_, raw, high.bitcast(F32), ALU.subtract)
                if last:
                    ins.then_inc(s_lo, 1)

            def job_lo(job):
                kind = job[0]
                if kind == "x1":
                    g = job[1]
                    ve.wait_ge(s_xin, 16 * (g + 1))
                    ve.wait_ge(s_dl, g + 1)
                    for q in range(TILES):
                        ve.tensor_tensor(x_res[:, q, :], x_res[:, q, :], down_ps[q][:], ALU.add).then_inc(s_x1, 1)
                    return
                if kind == "act":
                    s = job[1]
                    k = cw(s % FC)
                    ve.wait_ge(s_silu, s + 1)
                    ve.tensor_tensor(act[0:k, s % 2, :], act[0:k, s % 2, :], gu_ps[s % 2][0:k, 1, :],
                                     ALU.mult).then_inc(s_mul, 1)
                    ve.wait_ge(s_hi, pair_no[job])
                    lo(act_hl[0:k, s % 2, 1, :], act[0:k, s % 2, :], act_hl[0:k, s % 2, 0, :])
                elif kind == "at":
                    ve.wait_ge(s_hi, pair_no[job])
                    lo(agu_t[:, 1, :, :], tr_gu_ps[:], agu_t[:, 0, :, :])
                elif kind == "adt":
                    a, b = AD_PIECES[job[2]]
                    ve.wait_ge(s_hi, pair_no[job])
                    for c0, c1 in spans(a, b):
                        k = cw(c0)
                        lo(ad_t[0:k, c0:c1, 1, :], tr_d_ps[0:k, c0 - a:c1 - a, :], ad_t[0:k, c0:c1, 0, :], c1 == b)
                elif kind == "t":
                    g = job[1]
                    ve.wait_ge(s_tg, 2 * (g + 1))
                    ve.tensor_tensor(t_raw[:], tg_ps[:], const("mask").unsqueeze(1).to_broadcast([P, 2, GROUP]),
                                     ALU.mult).then_inc(s_mask, 1)
                    ve.wait_ge(s_hi, pair_no[job])
                    lo(t_hl[:, g % 2, 1, :, :], t_raw[:], t_hl[:, g % 2, 0, :, :])
                elif kind == "td":
                    g = job[1]
                    ve.wait_ge(s_d, FC * (g + 1))
                    ve.tensor_tensor(t_raw[:, 0, :], td_ps[:, 0:GROUP], const("mask"), ALU.mult).then_inc(s_mask, 1)
                    ve.wait_ge(s_hi, pair_no[job])
                    lo(td_hl[:, 1, :], t_raw[:, 0, :], td_hl[:, 0, :])
                elif kind == "b":
                    s = job[1]
                    w = 2 * cw(s % FC)
                    ve.wait_ge(s_hi, pair_no[job])
                    lo(b_sel[:, s % 2, 1, 0:w], raw_b(s), b_sel[:, s % 2, 0, 0:w])
                else:
                    ve.wait_ge(s_hi, pair_no[job])
                    raw, h, l = outputs_of(job)
                    lo(l, raw, h)

            def add_x2(t):
                ve.wait_ge(s_l1, t + 1)
                if t >= 3:
                    ve.wait_ge(s_x3, t - 2)
                ve.tensor_tensor(x2[:, t % 3, :], x1[:, t % 2, :], l1_ps[:], ALU.add).then_inc(s_x2, 1)

            def low_x2t(t):
                ve.wait_ge(s_x2thi, t + 1)
                ve.tensor_tensor(x2t_hl[:, t % 2, 1, :, :], x2t_ps[:], x2t_hl[:, t % 2, 0, :, :].bitcast(F32),
                                 ALU.subtract).then_inc(s_x2tlo, 1)

            for s in range(-1, STEPS + 2):
                for job in lane_jobs(s):
                    job_lo(job)
                if s == STEPS - 2:
                    add_x2(0)
                    ve.wait_ge(s_whi, 1)
                    ve.tensor_tensor(w2ra_hl[:, 1, :, :], w_raw[:, 0:HC * L2_COLS].rearrange("p (c o) -> p c o", c=HC),
                                     w2ra_hl[:, 0, :, :].bitcast(F32), ALU.subtract)
                    ve.tensor_tensor(b2_hl[:, 1, :], w_raw[:, HC * L2_COLS:], b2_hl[:, 0, :].bitcast(F32),
                                     ALU.subtract).then_inc(s_wlo, 1)
                if s == STEPS - 1:
                    ve.tensor_tensor(lang5[:], const("iota").unsqueeze(1).to_broadcast([P, NT, EXPERTS]),
                                     sel[:, 2, :].unsqueeze(2).to_broadcast([P, NT, EXPERTS]),
                                     ALU.is_equal).then_inc(s_lang, 1)
                    ve.wait_ge(s_lang, 1)
                    ve.tensor_scalar(lang5[:], lang5[:], LANG_BIAS, None, ALU.mult).then_inc(s_lang, 1)
                    low_x2t(0)

            chain = [0]

            def link(ins):
                chain[0] += 1
                ins.then_inc(s_dve, 1)
                ve.wait_ge(s_dve, chain[0])

            def routing_parts(t):
                r = route[:, t % 2, :]
                return (r[:, 0:8], r[:, 8:16], r[:, 16:17], r[:, 17:18], r[:, 18:19], r[:, 19:20], r[:, 20:21],
                        r[:, 24:32], r[:, 32:40], r[:, 40:48])

            def route_top(t):
                logits, top, gap, _, _, _, _, ids, _, _ = routing_parts(t)
                ve.wait_ge(s_base, t + 1)
                if t == 0:
                    ve.wait_ge(s_lang, 2)
                link(ve.tensor_tensor(logits, logits_of(t), lang5[:, t, :], ALU.add))
                link(ve.max(top, logits))
                ve.tensor_tensor(gap, top[:, 0:1], top[:, 1:2], ALU.subtract).then_inc(s_gap, 1)
                link(ve.max_index(order[:, t % 2, :], top, logits))
                link(ve.tensor_copy(ids, order[:, t % 2, :]))

            def route_gates(t):
                _, _, _, e, e1, w0, w1, ids, g0, g1 = routing_parts(t)
                ve.wait_ge(s_exp, t + 1)
                link(ve.tensor_scalar(e1, e, 1.0, 1.0 / SCALING, ALU.add, ALU.mult))
                link(ve.reciprocal(w0, e1))
                link(ve.tensor_tensor(w1, w0, e, ALU.mult))
                ve.tensor_scalar(g0, const("iota"), ids[:, 0:1], w0, ALU.is_equal, ALU.mult)
                link(ve.tensor_scalar(g1, const("iota"), ids[:, 1:2], w1, ALU.is_equal, ALU.mult))
                link(ve.tensor_tensor(g0, g0, g1, ALU.add))
                if t >= 2:
                    ve.wait_ge(s_hgt, t - 1)
                ve.tensor_tensor(hg[:, t % 2, :].rearrange("p (e r) -> p e r", r=RANK), h_of(t),
                                 g0.unsqueeze(2).to_broadcast([P, EXPERTS, RANK]), ALU.mult).then_inc(s_hg, 1)

            def low_hgt(t):
                ve.wait_ge(s_hgthi, t + 1)
                ve.tensor_tensor(hgt_hl[:, t % 2, 1, :], hgt_ps[:, 0:P], hgt_hl[:, t % 2, 0, :].bitcast(F32),
                                 ALU.subtract).then_inc(s_hgtlo, 1)

            def add_x3(t):
                ve.wait_ge(s_l2, t + 1)
                if t >= 3:
                    ve.wait_ge(s_y, t - 2)
                ve.tensor_tensor(x3[:, t % 3, :], x2[:, t % 3, :], base_of(t), ALU.add).then_inc(s_x3, 1)

            def add_y(t):
                ve.wait_ge(s_l3, t + 1)
                if t >= 2:
                    ve.wait_ge(s_out[t % 2], 16 * (t // 2))
                ve.tensor_tensor(y[:, t % 2, :], x3[:, t % 3, :], l3_ps[:], ALU.add).then_inc(s_y, 1)

            add_x2(1)
            for i in range(NT + 2):
                if 1 <= i <= NT:
                    low_hgt(i - 1)
                if i < NT:
                    route_top(i)
                if i + 1 < NT:
                    low_x2t(i + 1)
                if 1 <= i <= NT:
                    add_x3(i - 1)
                if i < NT:
                    route_gates(i)
                if i + 2 < NT:
                    add_x2(i + 2)
                if i >= 2:
                    add_y(i - 2)

        @block.tensor
        def _(pe):
            def product(out_, stationary, moving, start, stop):
                pe.matmul(out_, stationary[0], moving[0], start=start, stop=False, skip_group_check=True)
                pe.matmul(out_, stationary[0], moving[1], start=False, stop=False, skip_group_check=True)
                return pe.matmul(out_, stationary[1], moving[0], start=False, stop=stop, skip_group_check=True)

            def transpose_agu(g, m):
                it = ("agu", g, m)
                wait_item(pe, it)
                if (g, m) == (0, 0):
                    pe.wait_ge(s_const, 64)
                else:
                    before = (g, 0) if m else (g - 1, 1)
                    pe.wait_ge(s_lo, s_lo_of(("at",) + before))
                for c in range(HC):
                    mm = pe.transpose(tr_gu_ps[:, c, :], slot(it)[:, c * P:(c + 1) * P], ident)
                mm.then_inc(s_tr, 1)

            def transpose_ad(g, n):
                it = ("ad", g, n)
                a, b = AD_PIECES[n]
                wait_item(pe, it)
                if (g, n) != (0, 0):
                    before = (g, n - 1) if n else (g - 1, len(AD_PIECES) - 1)
                    pe.wait_ge(s_lo, s_lo_of(("adt",) + before))
                for c in range(a, b):
                    at = (c - a) * P
                    mm = pe.transpose(tr_d_ps[0:cw(c), c - a, :], slot(it)[:, at:at + cw(c)], ident)
                mm.then_inc(s_tr, 1)

            def x_a(g, m):
                if m == 0:
                    pe.wait_ge(s_lo, s_lo_of(("x", g, 1)))
                pe.wait_ge(s_lo, s_lo_of(("at", g, m)))
                if m == 0 and g >= 1:
                    pe.wait_ge(s_mask, mask_no(("t", g - 1)))
                for c in range(HC):
                    mm = product(tg_ps[:, m, :], (agu_t[:, 0, c, :], agu_t[:, 1, c, :]),
                                 (xt[:, g % 2, c, 0, :], xt[:, g % 2, c, 1, :]), c == 0, c == HC - 1)
                mm.then_inc(s_tg, 1)

            def gate_up_base(s, m):
                g, f = divmod(s, FC)
                w = cw(f)
                if s >= 2 and m == 0:
                    pe.wait_ge(s_mul, s - 1)
                if g == 0:
                    pe.wait_ge(s_lo, s_lo_of(("wgu", f, m)))
                for c in range(HC):
                    if f == 0 and m == 0 and c % (HC // 2) == 0:
                        pe.wait_ge(s_lo, s_lo_of(("x", g, c // (HC // 2))))
                    cols = slice(c * w, (c + 1) * w)
                    product(gu_ps[s % 2][0:w, m, :], (wgu_at(f, m, 0)[:, cols], wgu_at(f, m, 1)[:, cols]),
                            (xt[:, g % 2, c, 0, :], xt[:, g % 2, c, 1, :]), m == 0 and c == 0, False)

            def gate_up_adapters(s):
                g, f = divmod(s, FC)
                w = cw(f)
                pe.wait_ge(s_lo, s_lo_of(("b", s)))
                if f == 0:
                    pe.wait_ge(s_lo, s_lo_of(("t", g)))
                for m in range(2):
                    cols = slice(m * w, (m + 1) * w)
                    mm = product(gu_ps[s % 2][0:w, m, :], (b_sel[:, s % 2, 0, cols], b_sel[:, s % 2, 1, cols]),
                                 (t_hl[:, g % 2, 0, m, :], t_hl[:, g % 2, 1, m, :]), False, m == 1)
                mm.then_inc(s_gu, 1)

            def down(s):
                g, f = divmod(s, FC)
                w = cw(f)
                pe.wait_ge(s_lo, s_lo_of(("act", s)))
                if g == 0:
                    pe.wait_ge(s_lo, s_lo_of(("wd", f)))
                for n, (a, b) in enumerate(AD_PIECES):
                    if f == a:
                        pe.wait_ge(s_lo, s_lo_of(("adt", g, n)))
                if f == 0 and g >= 1:
                    pe.wait_ge(s_x1, TILES * g)
                    pe.wait_ge(s_mask, mask_no(("td", g - 1)))
                a_hi, a_lo = act_hl[0:w, s % 2, 0, :], act_hl[0:w, s % 2, 1, :]
                for q in range(TILES):
                    rows = slice(q * P, (q + 1) * P)
                    product(down_ps[q][:], (a_hi[:, rows], a_lo[:, rows]), (wd_sb[0:w, f, 0, :], wd_sb[0:w, f, 1, :]),
                            f == 0, False)
                product(td_ps[:, 0:GROUP], (ad_t[0:w, f, 0, :], ad_t[0:w, f, 1, :]), (a_hi, a_lo), f == 0,
                        f == FC - 1).then_inc(s_d, 1)

            def down_adapters(g):
                pe.wait_ge(s_lo, max(s_lo_of(("td", g)), s_lo_of(("bd", g))))
                for q in range(TILES):
                    rows = slice(q * P, (q + 1) * P)
                    mm = product(down_ps[q][:], (td_hl[:, 0, rows], td_hl[:, 1, rows]),
                                 (bd_hl[:, 0, :], bd_hl[:, 1, :]), False, True)
                mm.then_inc(s_dl, 1)

            def mix(bank, t, m, x_hl):
                return product(bank, (bd13_hl[:, t % BD, 0, m, :], bd13_hl[:, t % BD, 1, m, :]),
                               (x_hl[:, t % 2, 0, :], x_hl[:, t % 2, 1, :]), True, True)

            def l1(t):
                pe.wait_ge(s_x1lo, t + 1)
                if t >= 1:
                    pe.wait_ge(s_x2, t)
                mix(l1_ps[:], t, 0, x1_hl).then_inc(s_l1, 1)

            def transpose_x2(t):
                pe.wait_ge(s_x2, t + 1)
                if t >= 1:
                    pe.wait_ge(s_x2tlo, t)
                for c in range(HC):
                    mm = pe.transpose(x2t_ps[:, c, :], x2[:, t % 3, c * P:(c + 1) * P], ident)
                mm.then_inc(s_x2t, 1)

            def l2_base(t, c0, c1):
                if c0 == 0:
                    pe.wait_ge(s_x2tlo, t + 1)
                    if t == 0:
                        pe.wait_ge(s_wlo, 1)
                    if t >= 2:
                        pe.wait_ge(s_x3, t - 1)
                        pe.wait_ge(s_hg, t - 1)
                    if t == 1:
                        pe.wait_ge(s_x1, TILES * NG)
                for c in range(c0, c1):
                    hi_, lo_ = x2t_hl[:, t % 2, 0, c, :], x2t_hl[:, t % 2, 1, c, :]
                    for n, (x_part, part) in enumerate(((hi_, 0), (hi_, 1), (lo_, 0))):
                        for half in range(2):
                            at = (BASE_AT, H)[half]
                            mm = pe.matmul(l2_ps[t % 2][:, at:at + L2_PART], x_part,
                                           w2ra_hl[:, part, c, half * L2_PART:(half + 1) * L2_PART],
                                           start=(c == 0 and n == 0), stop=(c == HC - 1 and n == 2),
                                           skip_group_check=True)
                if c1 == HC:
                    mm.then_inc(s_base, 1)

            def transpose_hg(t):
                pe.wait_ge(s_hg, t + 1)
                if t >= 1:
                    pe.wait_ge(s_hgtlo, t)
                pe.transpose(hgt_ps[:, 0:P], hg[:, t % 2, :], ident).then_inc(s_hgt, 1)

            def experts(t):
                pe.wait_ge(s_hgtlo, t + 1)
                for a, b in ((0, L2_PART), (L2_PART, H)):
                    mm = product(l2_ps[t % 2][:, BASE_AT + a:BASE_AT + b],
                                 (hgt_hl[:, t % 2, 0, :], hgt_hl[:, t % 2, 1, :]),
                                 (b2_hl[:, 0, a:b], b2_hl[:, 1, a:b]), False, True)
                mm.then_inc(s_l2, 1)

            def l3(t):
                pe.wait_ge(s_x3lo, t + 1)
                if t >= 1:
                    pe.wait_ge(s_y, t)
                mix(l3_ps[:], t, 1, x3_hl).then_inc(s_l3, 1)

            gate_up_base(0, 0)
            gate_up_base(0, 1)
            for m in range(2):
                transpose_agu(0, m)
                gate_up_base(1, m)
                x_a(0, m)

            for s in range(STEPS):
                g, f = divmod(s, FC)
                for m in range(2):
                    if s >= 2:
                        gate_up_base(s, m)
                    if m == 0 and f == 1 and g > 0:
                        down_adapters(g - 1)
                gate_up_adapters(s)
                if s > 0:
                    down(s - 1)
                for kind, gg, n in pe_side(s):
                    {"at": transpose_agu, "tg": x_a, "adt": transpose_ad}[kind](gg, n)
                if s == STEPS - 2:
                    l1(0)
            transpose_x2(0)
            down(STEPS - 1)
            l1(1)
            l2_base(0, 0, HC // 2)
            down_adapters(NG - 1)
            l2_base(0, HC // 2, HC)
            transpose_x2(1)
            l1(2)
            for i in range(1, NT + 2):
                if i < NT:
                    l2_base(i, 0, HC - 1)
                if i - 1 < NT:
                    transpose_hg(i - 1)
                if i < NT:
                    l2_base(i, HC - 1, HC)
                if i + 1 < NT:
                    transpose_x2(i + 1)
                if i - 1 < NT:
                    experts(i - 1)
                if i >= 2:
                    l3(i - 2)
                if i + 2 < NT:
                    l1(i + 2)

N_IDX = 3 * 2 + 2


def spans(a, b):
    return [(a, b)] if b < FC else [(a, FC - 1), (FC - 1, FC)]


def mask_no(job):
    order = [j for s in range(-1, STEPS + FC) for j in lane_jobs(s) if j[0] in ("t", "td")]
    return order.index(job) + 1


def kernel(**inputs):
    import concourse.bacc as bacc
    from concourse.bass_utils import run_bass_kernel_spmd

    a = {k: np.asarray(v) for k, v in inputs.items()}

    def chunked_t(w, width):
        t = w.T.reshape(HC, P, -1)
        return [t[:, :, c:c + width].transpose(1, 0, 2).reshape(P, -1) for c in range(0, t.shape[2], width)]

    rows = a["x"].reshape(ROWS, H)
    wgu = [m for pair in zip(chunked_t(a["L0_cond_W_gate"], P), chunked_t(a["L0_cond_W_up"], P)) for m in pair]
    ab = ADAPTERS * RANK
    b_gate, b_up = (a[f"L0_cond_B_{k}"][0].transpose(0, 2, 1).reshape(ab, F) for k in ("gate", "up"))
    a_down = a["L0_cond_A_down"][0].reshape(ab, F)
    arrays = {
        "x_t": rows.T.reshape(HC, P, NG, GROUP).transpose(1, 2, 0, 3).reshape(P, NG, HC * GROUP),
        "x_rows": rows,
        "it_lora": a["itok_B_2_6"], "it_cond": a["itok_B_0_15"], "it_lang": a["itok_B_0_7"],
        "wgu": np.concatenate(wgu, axis=1),
        "wd": a["L0_cond_W_down"].T,
        "a_gate": a["L0_cond_A_gate"][0].reshape(ab, H),
        "a_up": a["L0_cond_A_up"][0].reshape(ab, H),
        "b_d": a["L0_cond_B_down"][0].transpose(0, 2, 1).reshape(ab, H),
        "w13": np.concatenate([a["L1_cond_weights"], a["L3_cond_weights"]], axis=2).reshape(CONDS * CH, 2 * CH),
        "w2ra_t": np.concatenate([a["L2_cond_W"], a["L2_cond_Wr"], a["L2_cond_A"].reshape(EXPERTS * RANK, H)]).T,
        "b2": a["L2_cond_B"].transpose(0, 2, 1).reshape(EXPERTS * RANK, H),
        "consts": CONSTS,
    }
    for n in range(PAIRS):
        chunks = [slice(c * P, c * P + cw(c)) for c in range(2 * n, min(2 * n + 2, FC))]
        arrays[f"b_gu{n}"] = np.concatenate([m[:, f] for f in chunks for m in (b_gate, b_up)], axis=1)
    for n, (c0, c1) in enumerate(AD_PIECES):
        arrays[f"a_d{n}"] = a_down[:, c0 * P:min(c1 * P, F)]
    arrays = {k: np.ascontiguousarray(v) for k, v in arrays.items()}

    nc = bacc.Bacc("TRN2", target_bir_lowering=False, num_devices=1)
    args = [nc.dram_tensor(k, v.shape, mybir.dt.from_np(v.dtype), kind="ExternalInput").ap()
            for k, v in arrays.items()]
    args.append(nc.dram_tensor("out", (ROWS, H), F32, kind="ExternalOutput").ap())
    bass_conditioned_residual_chain(nc, *args)
    r = run_bass_kernel_spmd(nc, [arrays], core_ids=[0])
    return r.results[0]["out"].reshape(BATCHES, CH, H)
```

```python
from contextlib import ExitStack

import numpy as np

import concourse.bass as bass
from concourse import mybir

F32 = mybir.dt.float32
F32R = mybir.dt.float32r
I32 = mybir.dt.int32
U32 = mybir.dt.uint32
ALU = mybir.AluOpType
ACT = mybir.ActivationFunctionType
AX_X = mybir.AxisListType.X

P = 128
BATCHES, CH, H = 64, 32, 512
F = 1376
RANK = 16
ADAPTERS = 16
CONDS = 16
EXPERTS = 8
LORA_SCALE = 0.5
LANG_BIAS = 5.0
SCALING = 2.0

ROWS = BATCHES * CH
HC = H // P
GROUP = 256
NG = ROWS // GROUP
GB = GROUP // CH
TILES = GROUP // P
NT = ROWS // P
TB = P // CH
FC = -(-F // P)
LASTW = F - (FC - 1) * P
STEPS = NG * FC
AD_PIECES = [(0, 4), (4, 8), (8, FC)]
PAIRS = -(-FC // 2)
HALF = H // 2
AD_HALF = TB * RANK // 2
D_COLS = HALF + AD_HALF
GU_BANKS = 3
AHEAD = 4
LOADS_AHEAD = 5
A_GU = HC * RANK
A_WORDS = 2 * A_GU + FC * RANK
BD = 6
H_HALF = EXPERTS * RANK // 2
L2_WIDTH = (HALF + H_HALF, HALF + H_HALF + EXPERTS)
L2_COLS = sum(L2_WIDTH)


def cw(c):
    return P if c < FC - 1 else LASTW


CONST_COLS = {}


def const_array():
    p = np.arange(P)
    blocks = {
        "ident": np.eye(P),
        "scale_rank": LORA_SCALE * (p[:, None] // RANK == np.arange(GB)[None, :]),
        "scale_ch": LORA_SCALE * (p[:, None] // CH == np.arange(TB)[None, :]),
        "is_rank": p[:, None] // RANK == np.arange(GB)[None, :],
        "is_ch": p[:, None] // CH == np.arange(TB)[None, :],
        "row_rank": (p % RANK)[:, None],
        "row_ch": (p % CH)[:, None],
        "row": p[:, None],
        "iota": np.broadcast_to(np.arange(EXPERTS), (P, EXPERTS)),
    }
    at = 0
    for name, b in blocks.items():
        CONST_COLS[name] = (at, at + b.shape[1])
        at += b.shape[1]
    return np.concatenate([b.astype(np.float32) for b in blocks.values()], axis=1)


CONSTS = const_array()


def plain_loads(s):
    g, f = divmod(s, FC)
    if s < 0:
        return ([("x", 0, 0), ("wgu", 0, 0), ("x", 0, 1), ("wgu", 0, 1)]
                + [("wgu", c, m) for c in range(1, GU_BANKS) for m in range(2)]
                + ["adapters first", ("wgu", GU_BANKS, 0), ("wgu", GU_BANKS, 1), ("wd", 0)]
                + [i for c in range(AHEAD, FC - 1) for i in (("wgu", c, 0), ("wgu", c, 1), ("wd", c - AHEAD + 1))]
                + [("x", 1, 0), ("x", 1, 1), ("wgu", FC - 1, 0), ("wgu", FC - 1, 1)]
                + [("wd", c) for c in range(FC - AHEAD, FC)])
    return [("x", g + 1, 0), ("x", g + 1, 1)] if f == 0 and 1 <= g < NG - 1 else []


def gathers(s):
    g, f = divmod(s, FC)
    if s < 0:
        return [("a", 0, b) for b in range(GB)] + [("b", 0, 0), ("b", 0, 1)]
    out = []
    first = s + 2 if s > 8 else s + 4 if s <= 6 else STEPS
    if first < STEPS and first % FC % 2 == 0:
        out.append(("b", first // FC, first % FC // 2))
    half = f - (3 if g == 0 else 0)
    if g + 1 < NG and half in (0, 1):
        out += [("a", g + 1, b) for b in range(half * GB // 2, (half + 1) * GB // 2)]
    if f == 6:
        out.append(("bd", g))
    return out


def x_a_jobs(s):
    g, f = divmod(s, FC)
    at = (5, 7) if g else (7, 9)
    return [(g + 1, at.index(f))] if g + 1 < NG and f in at else []


def lane_jobs(s):
    g, f = divmod(s, FC)
    if s < 0:
        return ([("x", 0, 0), ("wgu", 0, 0), ("x", 0, 1), ("wgu", 0, 1)]
                + [("wgu", c, m) for c in range(1, GU_BANKS) for m in range(2)]
                + [("at", 0, 0), ("at", 0, 1), ("adt", 0, 0), ("b", 0, 0)]
                + [("wgu", GU_BANKS, 0), ("t", 0), ("b", 0, 1), ("wgu", GU_BANKS, 1), ("wd", 0)])
    jobs = []
    if f == 1 and g > 0:
        jobs.append(("x1", g - 1))
    if s < STEPS:
        jobs.append(("act", s))
    if f == 0 and 0 < g < NG:
        jobs.append(("adt", g, 2))
    if f == 0 and g > 0:
        jobs.append(("td", g - 1))
    if s >= STEPS:
        return jobs
    if s == 2:
        jobs.append(("b", 0, 2))
    elif s >= 4 and s + 1 < STEPS and (s + 1) % FC % 2 == 0:
        jobs.append(("b", (s + 1) // FC, (s + 1) % FC // 2))
    if g == 0:
        jobs += [("wd", f + 1)] if f + 1 < FC else []
        jobs += [("wgu", f + AHEAD, m) for m in range(2)] if f + AHEAD < FC else []
        jobs += {3: [("adt", 0, 1), ("adt", 0, 2)]}.get(f, [])
    if g + 1 < NG:
        n = g + 1
        jobs += {7: [("adt", n, 0)], 9: [("adt", n, 1)]}.get(f, [])
        jobs += {2 if g else 5: [("x", n, 0)], 3 if g else 6: [("x", n, 1)]}.get(f, [])
        jobs += {f0 - 1: [("at",) + j] for f0 in range(1, FC) for j in x_a_jobs(g * FC + f0)}.get(f, [])
        jobs += {8 if g else 9: [("t", n)]}.get(f, [])
    if f == 8:
        jobs.append(("bd", g))
    return jobs


def bass_conditioned_residual_chain(nc, x_t, x_rows, it_lora, it_cond, it_lang, wgu, wd, a_all, b_d,
                                    w13, w2ra_t, b2, consts, *rest):
    b_gu, rest = rest[:PAIRS], rest[PAIRS:]
    (out,) = rest

    pairs = [j for s in range(-1, STEPS + FC) for j in lane_jobs(s) if j[0] != "x1"]
    hi_no = {j: n + 1 for n, j in enumerate(pairs)}
    lo_no = {j: n + 1 for n, j in enumerate(j for j in pairs if j[0] != "wd")}

    with ExitStack() as ctx:
        def sb(name, shape, dt=F32, stack=ctx):
            return stack.enter_context(nc.sbuf_tensor(name, [P, *shape], dt))

        def ps(name, shape, stack=ctx):
            return stack.enter_context(nc.psum_tensor(name, [P, *shape], F32))

        def sb_raw(name, shape, stack):
            with nc.sbuf_tensor(name + "_raw", [P, *shape], F32) as raw:
                pass
            return sb(name, shape, F32R, stack), raw

        def sem(name):
            return ctx.enter_context(nc.semaphore(name))

        const_sb = sb("const_sb", [CONSTS.shape[1]])
        itok = sb("itok", [3, BATCHES], I32)
        picked = sb("picked", [BATCHES])
        sel = sb("sel", [3, NT])
        warm = sb("warm", [1])
        idx_batch = sb("idx_batch", [BATCHES], U32)
        idx_rank = sb("idx_rank", [NG], U32)
        idx_ch = sb("idx_ch", [NT], U32)
        x_scratch = nc.dram_tensor("x_after_l0", [ROWS, H], F32, kind="Internal").ap()

        def const(name):
            a, b = CONST_COLS[name]
            return const_sb[:, a:b]

        ident = const("ident")

        mem_a = ExitStack()
        a_raw = sb("a_raw", [GB, A_WORDS], F32, mem_a)
        agu_t = sb("agu_t", [2, HC, P], F32R, mem_a)
        xt0, xt0_raw = sb_raw("xt0", [2, HC, GROUP], mem_a)
        wgu_sb, wgu_sb_raw = sb_raw("wgu_sb", [(FC - 1) * 4 * H + 4 * HC * LASTW], mem_a)
        wd_sb, wd_sb_raw = sb_raw("wd_sb", [FC, 2, 2, AD_HALF + HALF + AD_HALF], mem_a)
        xt1, xt1_raw = sb_raw("xt1", [2, HC, GROUP], mem_a)
        xt, xt_raw = (xt0, xt1), (xt0_raw, xt1_raw)
        act = sb("act", [2, GROUP], F32, mem_a)
        act_hl = sb("act_hl", [2, 2, GROUP], F32R, mem_a)
        b_sel, b_sel_raw = sb_raw("b_sel", [2, 2, 4 * P], mem_a)
        t_raw = sb("t_raw", [2, GROUP], F32, mem_a)
        t_hl = sb("t_hl", [2, 2, 2, GROUP], F32R, mem_a)
        td = sb("td", [TILES, P], F32, mem_a)
        td_hl = sb("td_hl", [2, GROUP], F32R, mem_a)
        bd_hl, bd_hl_raw = sb_raw("bd_hl", [2, H], mem_a)
        with nc.sbuf_tensor("agu_t_up0", [P, 2, HC, P], F32R) as agu_t_up0:
            pass
        x_res = sb("x_res", [TILES, H], F32, mem_a)
        mem_a.close()

        banks_a = ExitStack()
        gu_ps = [ps(f"gu_ps{i}", [2, GROUP], banks_a) for i in range(GU_BANKS)]
        down_ps = [ps(f"down_ps{i}", [2, H], banks_a) for i in range(TILES)]
        tg_ps = ps("tg_ps", [2, GROUP], banks_a)
        banks_a.close()

        w13_raw = sb("w13_raw", [NT, 2 * CH])
        x1 = sb("x1", [2, H])
        bd_raw = sb("bd_raw", [2, 2, P])
        x1_hl = sb("x1_hl", [2, 2, H], F32R)
        bd13_hl = sb("bd13_hl", [BD, 2, 2, P], F32R)
        w_raw = sb("w_raw", [HC * L2_COLS + H])
        w2ra_hl = sb("w2ra_hl", [2, HC, L2_COLS], F32R)
        b2_hl = sb("b2_hl", [2, H], F32R)
        lang5 = sb("lang5", [NT, EXPERTS])
        x2 = sb("x2", [3, H])
        x2t_hl = sb("x2t_hl", [2, 2, HC, P], F32R)
        route = sb("route", [2, 64])
        order = sb("order", [2, EXPERTS], U32)
        hg = sb("hg", [2, P])
        hgt_hl = sb("hgt_hl", [2, 2, P], F32R)
        x3 = sb("x3", [3, H])
        x3_hl = sb("x3_hl", [2, 2, H], F32R)
        y = sb("y", [2, H])

        l2_ps = [ps(f"l2_ps{i}", [2, H]) for i in range(2)]
        hgt_ps = ps("hgt_ps", [H])
        l1_ps = ps("l1_ps", [H])
        l3_ps = ps("l3_ps", [H])
        x2t_ps = ps("x2t_ps", [HC, P])

        def pieces(t):
            return [(0, H)] if t < NT - 1 else [(0, HALF), (HALF, H)]

        def l3_of(t, n):
            a, b = pieces(t)[n]
            return (l3_ps if t < NT - 1 else (l1_ps, hgt_ps)[n])[:, a:b]

        def l1_of(t):
            return gu_ps[t][:].rearrange("p m n -> p (m n)") if t < 3 else l1_ps[:]

        def halves(v, a, b):
            return v[:, a:b].rearrange("p (j n) -> p j n", n=HALF)

        def base_of(t, a, b):
            return l2_ps[t % 2][:, a // HALF:b // HALF, 0:HALF]

        def logits_of(t):
            at = L2_WIDTH[0]
            return l2_ps[t % 2][:, 1, at:at + EXPERTS]

        def h_of(t):
            return l2_ps[t % 2][:, :, HALF:HALF + H_HALF].rearrange("p j (e r) -> p j e r", r=RANK)

        s_const = sem("s_const")
        s_const2 = sem("s_const2")
        s_warm = sem("s_warm")
        s_zero = sem("s_zero")
        s_idx = sem("s_idx")
        s_wgu_in = [[sem(f"s_wgu_in{c}_{m}") for m in range(2)] for c in range(FC)]
        s_wd_in = [sem(f"s_wd_in{c}") for c in range(FC)]
        s_xt_in = [[sem(f"s_xt_in{i}_{h}") for h in range(2)] for i in range(2)]
        s_a_in = sem("s_a_in")
        s_b_in = [sem(f"s_b_in{i}") for i in range(2)]
        s_bd_in = sem("s_bd_in")
        s_xin = sem("s_xin")
        s_xout = sem("s_xout")
        s_tg = sem("s_tg")
        s_gu = sem("s_gu")
        s_tdt = sem("s_tdt")
        s_d = sem("s_d")
        s_dl = sem("s_dl")
        s_silu = sem("s_silu")
        s_mul = sem("s_mul")
        s_hi = sem("s_hi")
        s_wdlo = sem("s_wdlo")
        s_lo = sem("s_lo")
        s_mask = sem("s_mask")
        s_x1 = sem("s_x1")
        s_w = sem("s_w")
        s_w13 = sem("s_w13")
        s_x1in = [sem(f"s_x1in{i}") for i in range(2)]
        s_whi = sem("s_whi")
        s_wlo = sem("s_wlo")
        s_lang = sem("s_lang")
        s_bd = sem("s_bd")
        s_bdhi = sem("s_bdhi")
        s_bdlo = sem("s_bdlo")
        s_x1hi = sem("s_x1hi")
        s_x1lo = sem("s_x1lo")
        s_l1 = sem("s_l1")
        s_x2 = sem("s_x2")
        s_x2t = sem("s_x2t")
        s_x2thi = sem("s_x2thi")
        s_x2tlo = sem("s_x2tlo")
        s_logits = sem("s_logits")
        s_base = sem("s_base")
        s_dve = sem("s_dve")
        s_gap = sem("s_gap")
        s_exp = sem("s_exp")
        s_hg = sem("s_hg")
        s_hgt = sem("s_hgt")
        s_hgthi = sem("s_hgthi")
        s_hgtlo = sem("s_hgtlo")
        s_l2 = sem("s_l2")
        s_x3 = sem("s_x3")
        s_x3hi = sem("s_x3hi")
        s_x3lo = sem("s_x3lo")
        s_l3 = sem("s_l3")
        s_y = sem("s_y")
        s_out = [sem(f"s_out{i}") for i in range(2)]

        def wgu_at(c, m, part, memory=wgu_sb):
            w = cw(c)
            at = c * 4 * H + (part * 2 + m) * HC * w
            return memory[:, at:at + HC * w]

        def pair_words(n):
            return 2 * (min((2 * n + 2) * P, F) - 2 * n * P)

        def pair_at(g, n):
            return g * PAIRS + n

        def parts(job):
            kind = job[0]
            if kind == "wgu":
                _, c, m = job
                return wgu_at(c, m, 1, wgu_sb_raw), wgu_at(c, m, 0), wgu_at(c, m, 1)
            if kind == "wd":
                c = job[1]
                k = cw(c)
                w = slice(AD_HALF, AD_HALF + HALF)
                return wd_sb_raw[0:k, c, 1, :, w], wd_sb[0:k, c, 0, :, w], wd_sb[0:k, c, 1, :, w]
            if kind == "x":
                _, g, h = job
                hc = slice(h * HC // 2, (h + 1) * HC // 2)
                return xt_raw[g % 2][:, 1, hc, :], xt[g % 2][:, 0, hc, :], xt[g % 2][:, 1, hc, :]
            if kind == "b":
                _, g, n = job
                k, w = pair_at(g, n) % 2, pair_words(n)
                return b_sel_raw[:, k, 1, 0:w], b_sel[:, k, 0, 0:w], b_sel[:, k, 1, 0:w]
            if kind == "bd":
                return bd_hl_raw[:, 1, :], bd_hl[:, 0, :], bd_hl[:, 1, :]
            raise ValueError(kind)

        def landing(it):
            kind = it[0]
            if kind == "wgu":
                return s_wgu_in[it[1]][it[2]], 16
            if kind == "wd":
                return s_wd_in[it[1]], 16
            if kind == "x":
                return s_xt_in[it[1] % 2][it[2]], 16 * (it[1] // 2 + 1)
            if kind == "b":
                k = pair_at(it[1], it[2])
                return s_b_in[k % 2], 16 * (k // 2 + 1)
            if kind == "bd":
                return s_bd_in, 16 * (it[1] + 1)
            raise ValueError(kind)

        def agu_of(g, m):
            return agu_t_up0 if (g, m) == (0, 1) else agu_t

        def a_of(job):
            kind, g, n = job
            if kind == "at":
                return [(a_raw[:, :, n * A_GU:(n + 1) * A_GU].rearrange("p b (c r) -> p c b r", r=RANK),
                         *[agu_of(g, n)[:, part, :, :].rearrange("p c (b r) -> p c b r", r=RANK)
                           for part in range(2)])]
            a, b = AD_PIECES[n]
            out = []
            for q in range(TILES):
                for half in range(2):
                    first = q * TB + half * TB // 2
                    cols = slice(q * D_COLS, q * D_COLS + AD_HALF)
                    raw = a_raw[:, first:first + TB // 2, 2 * A_GU + a * RANK:2 * A_GU + b * RANK]
                    out.append((raw.rearrange("p b (c r) -> p c b r", r=RANK),
                                *[wd_sb[:, a:b, part, half, cols].rearrange("p c (b r) -> p c b r", r=RANK)
                                  for part in range(2)]))
            return out

        def down_of(q):
            at = (1 - q) * AD_HALF
            return down_ps[q][:, :, at:at + HALF]

        def td_of(q):
            at = q * HALF
            return down_ps[q][:, :, at:at + AD_HALF]

        def w2_parts(n):
            if n < HC:
                return w_raw[:, n * L2_COLS:(n + 1) * L2_COLS], w2ra_hl[:, 0, n, :], w2ra_hl[:, 1, n, :]
            return w_raw[:, HC * L2_COLS:], b2_hl[:, 0, :], b2_hl[:, 1, :]

        def step_after(last):
            words = 0
            for tensor in (w13_raw, x1, bd_raw, x1_hl, bd13_hl, w_raw, w2ra_hl, b2_hl):
                words += int(np.prod(tensor.shape[1:]))
                if tensor is last:
                    break
            words -= GB * A_WORDS + 2 * HC * P + 2 * HC * GROUP
            return STEPS - FC + -(-words // (4 * H))

        def s_lo_of(job):
            return lo_no[job]

        td_t = tg_ps[:, 0, :]

        block = ctx.enter_context(nc.Block())

        @block.sync
        def _(sp):
            def store_group(g):
                sp.wait_ge(s_x1, TILES * (g + 1))
                sp.dma_start(x_scratch[g * GROUP:(g + 1) * GROUP, :].rearrange("(q p) h -> p q h", p=P),
                             x_res[:]).then_inc(s_xout, 16)

            def load(it):
                if it == "adapters first":
                    sp.wait_ge(s_a_in, 16 * GB)
                    return
                kind = it[0]
                dst = parts(it)[0]
                if kind == "wgu":
                    _, c, m = it
                    if c > LOADS_AHEAD and m == 0:
                        sp.wait_ge(s_gu, c - LOADS_AHEAD)
                    at = c * 2 * H + m * HC * cw(c)
                    src = wgu[:, at:at + HC * cw(c)]
                elif kind == "wd":
                    src = wd[it[1] * P:it[1] * P + cw(it[1]), :].rearrange("p (j n) -> p j n", n=HALF)
                else:
                    _, g, h = it
                    if g >= 2:
                        sp.wait_ge(s_gu, (g - 1) * FC)
                    src = x_t[:, g, h * H:(h + 1) * H].rearrange("p (c n) -> p c n", n=GROUP)
                sp.dma_start(dst, src).then_inc(landing(it)[0], 16)

            sp.dma_start(const_sb[:], consts).then_inc(s_const, 16)
            for s in range(-1, STEPS):
                g, f = divmod(s, FC)
                if f == 2 and g > 0:
                    store_group(g - 1)
                for it in plain_loads(s):
                    load(it)
                if s == 0:
                    sp.dma_start(itok[:, 1, :], it_cond.partition_broadcast(P)).then_inc(s_const2, 16)
                    sp.dma_start(itok[:, 2, :], it_lang.partition_broadcast(P)).then_inc(s_const2, 16)
                if f == 4:
                    if g == 0:
                        sp.wait_ge(s_tg, 2)
                    sp.wait_ge(s_xout, 16 * g)
                    sp.dma_start(x_res[:], x_rows[g * GROUP:(g + 1) * GROUP, :]
                                 .rearrange("(q p) h -> p q h", p=P)).then_inc(s_xin, 16)
            def load_tile(t):
                if t >= 2:
                    sp.wait_ge(s_x2, t - 1)
                sp.dma_start(x1[:, t % 2, :], x_scratch[t * P:(t + 1) * P, :]).then_inc(s_x1in[t % 2], 16)

            sp.wait_ge(s_lo, s_lo_of(("adt", NG - 1, len(AD_PIECES) - 1)))
            load_tile(0)
            load_tile(1)
            sp.wait_ge(s_gu, step_after(w_raw))
            sp.dma_start(w_raw[:, 0:HC * L2_COLS].rearrange("p (c o) -> p c o", c=HC),
                         w2ra_t.rearrange("(c p) o -> p c o", p=P)).then_inc(s_w, 16)
            sp.dma_start(w_raw[:, HC * L2_COLS:], b2).then_inc(s_w, 16)
            load_tile(2)
            load_tile(3)
            store_group(NG - 1)
            for t in range(4, NT + 5):
                if t == (NG - 1) * TILES:
                    sp.wait_ge(s_xout, 16 * NG)
                if t < NT:
                    load_tile(t)
                if t >= 5:
                    u = t - 5
                    for n, (a, b) in enumerate(pieces(u)):
                        sp.wait_ge(s_y, u + n + 1)
                        sp.dma_start(out[u * P:(u + 1) * P, a:b], y[:, u % 2, a:b]).then_inc(s_out[u % 2], 16)
            for i in range(2):
                sp.wait_ge(s_out[i], 16 * sum(len(pieces(t)) for t in range(i, NT, 2)))

        @block.gpsimd
        def _(pool):
            def gather(dst, table, idx, s):
                nc.gpsimd.indirect_dma_start(
                    out=dst, out_offset=None, in_=table,
                    in_offset=bass.IndirectOffsetOnAxis(ap=idx, axis=0)).then_inc(s, 16)

            def gather_item(it):
                kind, g = it[0], it[1]
                if kind == "a":
                    if it[2] == 0 and g == 0:
                        pool.wait_ge(s_idx, IDX_BATCH)
                    elif it[2] == 0:
                        pool.wait_ge(s_lo, s_lo_of(("adt", g - 1, len(AD_PIECES) - 1)))
                    at = g * GB + it[2]
                    gather(a_raw[:, it[2], :], a_all, idx_batch[:, at:at + 1], s_a_in)
                    return
                if kind == "b":
                    k = pair_at(g, it[2])
                    if k == 0:
                        pool.wait_ge(s_idx, IDX_RANK)
                    if k >= 2:
                        pool.wait_ge(s_gu, first_step(k - 1))
                    table = b_gu[it[2]]
                else:
                    if g >= 1:
                        pool.wait_ge(s_dl, TILES * g)
                    table = b_d
                gather(parts(it)[0], table, idx_rank[:, g:g + 1], landing(it)[0])

            def block_diagonals(t):
                if t >= 2:
                    pool.wait_ge(s_bdlo, t - 1)
                if t == 0:
                    pool.wait_ge(s_gu, step_after(bd13_hl))
                for m in range(2):
                    ins = pool.tensor_tensor(
                        bd_raw[:, t % 2, m, :].rearrange("p (b d) -> p b d", b=TB),
                        w13_raw[:, t, m * CH:(m + 1) * CH].unsqueeze(1).to_broadcast([P, TB, CH]),
                        const("is_ch").unsqueeze(2).to_broadcast([P, TB, CH]), ALU.mult)
                ins.then_inc(s_bd, 1)

            def lows(t):
                pool.wait_ge(s_bdhi, t + 1)
                pool.tensor_tensor(bd13_hl[:, t % BD, 1, :, :], bd_raw[:, t % 2, :, :],
                                   bd13_hl[:, t % BD, 0, :, :].bitcast(F32), ALU.subtract).then_inc(s_bdlo, 1)
                pool.wait_ge(s_x1hi, t + 1)
                pool.tensor_tensor(x1_hl[:, t % 2, 1, :], x1[:, t % 2, :],
                                   x1_hl[:, t % 2, 0, :].bitcast(F32), ALU.subtract).then_inc(s_x1lo, 1)

            def low_x3(t):
                pool.wait_ge(s_x3hi, t + 1)
                pool.tensor_tensor(x3_hl[:, t % 2, 1, :], x3[:, t % 3, :],
                                   x3_hl[:, t % 2, 0, :].bitcast(F32), ALU.subtract).then_inc(s_x3lo, 1)

            for s in range(-1, STEPS):
                first = [it for it in gathers(s) if it[0] == "b" or s < 0]
                for it in first:
                    gather_item(it)
                for job in lane_jobs(s):
                    if job[0] == "wd":
                        raw, h, l = parts(job)
                        pool.wait_ge(s_hi, hi_no[job])
                        pool.tensor_tensor(l, raw, h.bitcast(F32), ALU.subtract).then_inc(s_wdlo, 1)
                for it in gathers(s)[len(first):]:
                    gather_item(it)
                n = s - (STEPS - FC + 1)
                if n == 0:
                    pool.wait_ge(s_idx, N_IDX)
                    pool.wait_ge(s_lo, s_lo_of(("adt", NG - 1, len(AD_PIECES) - 1)))
                if n >= 0:
                    for t in range(4 * n, min(4 * n + 4, NT)):
                        gather(w13_raw[:, t, :], w13, idx_ch[:, t:t + 1], s_w13)
                if s == STEPS - 6:
                    pool.wait_ge(s_w13, 16 * NT)
                    block_diagonals(0)
                    block_diagonals(1)
                    lows(0)
                    lows(1)
            block_diagonals(2)
            lows(2)
            for t in range(3, NT + 4):
                if t < NT:
                    block_diagonals(t)
                if 4 <= t < NT + 3:
                    low_x3(t - 4)
                if t < NT:
                    lows(t)

        @block.scalar
        def _(sc):
            sc.dma_start(itok[:, 0, :], it_lora.partition_broadcast(P)).then_inc(s_const, 16)

            sc.wait_ge(s_warm, 1)
            sc.activation(warm[:], warm[:], ACT.Silu)

            def hi(out_, in_):
                sc.copy(out_, in_).then_inc(s_hi, 1)

            def hi_all(operands):
                for raw, h, _ in operands:
                    ins = sc.copy(h, raw)
                ins.then_inc(s_hi, 1)

            def job_hi(job):
                kind = job[0]
                if kind == "x1":
                    return
                if kind == "act":
                    s = job[1]
                    f = s % FC
                    k = cw(f)
                    sc.wait_ge(s_gu, s + 1)
                    if s >= 2:
                        sc.wait_ge(s_lo, s_lo_of(("act", s - 2)))
                    sc.activation(act[0:k, s % 2, :], gu_ps[s % GU_BANKS][0:k, 0, :], ACT.Silu).then_inc(s_silu, 1)
                    sc.wait_ge(s_mul, s + 1)
                    if s >= 2:
                        sc.wait_ge(s_d, s - 1)
                    hi(act_hl[0:k, s % 2, 0, :], act[0:k, s % 2, :])
                elif kind == "at":
                    _, g, m = job
                    sc.wait_ge(s_a_in, 16 * GB * (g + 1))
                    if g > 0:
                        sc.wait_ge(s_tg, 2 * g + m)
                    hi_all(a_of(job))
                elif kind == "adt":
                    _, g, n = job
                    if g >= 1:
                        sc.wait_ge(s_d, (g - 1) * FC + AD_PIECES[n][1])
                    hi_all(a_of(job))
                elif kind == "t":
                    g = job[1]
                    sc.wait_ge(s_mask, mask_no(("t", g)))
                    if g >= 2:
                        sc.wait_ge(s_gu, (g - 1) * FC)
                    hi(t_hl[:, g % 2, 0, :, :], t_raw[:])
                elif kind == "td":
                    g = job[1]
                    sc.wait_ge(s_tdt, g + 1)
                    if g >= 1:
                        sc.wait_ge(s_dl, TILES * g)
                    hi(td_hl[:, 0, :], td_t)
                else:
                    landed, value = landing(job)
                    sc.wait_ge(landed, value)
                    raw, h, _ = parts(job)
                    hi(h, raw)

            def high_x2t(t):
                sc.wait_ge(s_x2t, t + 1)
                if t >= 2:
                    sc.wait_ge(s_base, t - 1)
                sc.copy(x2t_hl[:, t % 2, 0, :, :], x2t_ps[:]).then_inc(s_x2thi, 1)

            def high_hgt(t):
                sc.wait_ge(s_hgt, t + 1)
                if t >= 2:
                    sc.wait_ge(s_l2, t - 1)
                sc.copy(hgt_hl[:, t % 2, 0, :], hgt_ps[:, 0:P]).then_inc(s_hgthi, 1)

            def high_x3(t):
                if t >= 2:
                    sc.wait_ge(s_l3, t - 1)
                for n, (a, b) in enumerate(pieces(t)):
                    sc.wait_ge(s_x3, t + n + 1)
                    sc.copy(x3_hl[:, t % 2, 0, a:b], x3[:, t % 3, a:b]).then_inc(s_x3hi, 1)

            def exponential(t):
                sc.wait_ge(s_gap, t + 1)
                sc.activation(route[:, t % 2, 17:18], route[:, t % 2, 16:17], ACT.Exp, scale=-1.0).then_inc(s_exp, 1)

            def highs(t):
                sc.wait_ge(s_bd, t + 1)
                if t >= BD:
                    sc.wait_ge(s_l3, t - BD + 1)
                sc.copy(bd13_hl[:, t % BD, 0, :, :], bd_raw[:, t % 2, :, :]).then_inc(s_bdhi, 1)
                sc.wait_ge(s_x1in[t % 2], 16 * (t // 2 + 1))
                if t >= 2:
                    sc.wait_ge(s_l1, t - 1)
                sc.copy(x1_hl[:, t % 2, 0, :], x1[:, t % 2, :]).then_inc(s_x1hi, 1)

            for s in range(-1, STEPS + 2):
                for job in lane_jobs(s):
                    job_hi(job)
                if s == STEPS - 6:
                    highs(0)
                    highs(1)
                if 0 <= s - (STEPS - 5) <= HC:
                    n = s - (STEPS - 5)
                    if n == 0:
                        sc.wait_ge(s_w, 32)
                        sc.wait_ge(s_gu, step_after(b2_hl))
                    raw, h, _ = w2_parts(n)
                    sc.copy(h, raw).then_inc(s_whi, 1)
                if s == STEPS - 2:
                    high_x2t(0)
                    highs(2)
                if s == STEPS - 1:
                    high_x2t(1)
            for i in range(NT + 1):
                if i >= 1:
                    high_hgt(i - 1)
                    if i + 1 < NT:
                        high_x2t(i + 1)
                if i < NT:
                    exponential(i)
                if 1 <= i < NT - 1:
                    high_x3(i - 1)
                if i + 3 < NT:
                    highs(i + 3)
            high_x3(NT - 2)
            high_x3(NT - 1)

        @block.vector
        def _(ve):
            sub = [0]

            def step(ins):
                sub[0] += 1
                ins.then_inc(s_idx, 1)
                ve.wait_ge(s_idx, sub[0])

            def pick(n, mask, k):
                t = BATCHES // k
                step(ve.tensor_tensor(picked[:].rearrange("p (t k) -> p t k", k=k),
                                      itok[:, n, :].rearrange("p (t k) -> p t k", k=k),
                                      const(mask).unsqueeze(1).to_broadcast([P, t, k]), ALU.mult))
                step(ve.tensor_reduce(sel[:, n, 0:t], picked[:].rearrange("p (t k) -> p t k", k=k), AX_X, ALU.add))

            def batch_indices():
                ve.wait_ge(s_const, 32)
                step(ve.tensor_scalar(idx_batch[:], itok[:, 0, :], float(P), const("row"), ALU.mult, ALU.add))
                assert sub[0] == IDX_BATCH

            def rank_indices():
                pick(0, "is_rank", GB)
                step(ve.tensor_scalar(idx_rank[:], sel[:, 0, 0:NG], float(RANK), const("row_rank"),
                                      ALU.mult, ALU.add))
                assert sub[0] == IDX_RANK

            def tile_indices():
                ve.wait_ge(s_const2, 32)
                pick(1, "is_ch", TB)
                step(ve.tensor_scalar(idx_ch[:], sel[:, 1, :], float(CH), const("row_ch"), ALU.mult, ALU.add))
                pick(2, "is_ch", TB)
                assert sub[0] == N_IDX

            def lo(out_, raw, high):
                ve.tensor_tensor(out_, raw, high.bitcast(F32), ALU.subtract).then_inc(s_lo, 1)

            def mask_td(g):
                ve.wait_ge(s_d, FC * (g + 1))
                if g == 0:
                    ve.wait_ge(s_zero, 1)
                else:
                    ve.wait_ge(s_tdt, g)
                for q in range(TILES):
                    own = slice(q * TB * RANK, (q + 1) * TB * RANK)
                    ins = ve.tensor_tensor(
                        td[:, q, own].rearrange("p (j b r) -> p j b r", j=2, r=RANK),
                        td_of(q).rearrange("p j (b r) -> p j b r", r=RANK),
                        const("scale_ch").rearrange("p (j b) -> p j b", j=2).unsqueeze(3).to_broadcast(
                            [P, 2, TB // 2, RANK]), ALU.mult)
                ins.then_inc(s_mask, 1)

            def job_lo(job):
                kind = job[0]
                if kind == "wd":
                    return
                if kind == "x1":
                    g = job[1]
                    ve.wait_ge(s_xin, 16 * (g + 1))
                    for q in range(TILES):
                        ve.wait_ge(s_dl, TILES * g + q + 1)
                        x_q = x_res[:, q, :].rearrange("p (j n) -> p j n", n=HALF)
                        ve.tensor_tensor(x_q, x_q, down_of(q), ALU.add).then_inc(s_x1, 1)
                    return
                if kind == "act":
                    s = job[1]
                    k = cw(s % FC)
                    ve.wait_ge(s_silu, s + 1)
                    ve.tensor_tensor(act[0:k, s % 2, :], act[0:k, s % 2, :], gu_ps[s % GU_BANKS][0:k, 1, :],
                                     ALU.mult).then_inc(s_mul, 1)
                    if s % FC == 0 and s > 0:
                        mask_td(s // FC - 1)
                    ve.wait_ge(s_hi, hi_no[job])
                    lo(act_hl[0:k, s % 2, 1, :], act[0:k, s % 2, :], act_hl[0:k, s % 2, 0, :])
                elif kind == "t":
                    g = job[1]
                    ve.wait_ge(s_tg, 2 * (g + 1))
                    ve.tensor_tensor(t_raw[:].rearrange("p m (b n) -> p m b n", n=CH),
                                     tg_ps[:].rearrange("p m (b n) -> p m b n", n=CH),
                                     const("scale_rank").unsqueeze(1).unsqueeze(3).to_broadcast([P, 2, GB, CH]),
                                     ALU.mult).then_inc(s_mask, 1)
                    ve.wait_ge(s_hi, hi_no[job])
                    lo(t_hl[:, g % 2, 1, :, :], t_raw[:], t_hl[:, g % 2, 0, :, :])
                elif kind == "td":
                    if job[1] == NG - 1:
                        mask_td(NG - 1)
                        route_top(0)
                    ve.wait_ge(s_hi, hi_no[job])
                    lo(td_hl[:, 1, :], td_t, td_hl[:, 0, :])
                else:
                    ve.wait_ge(s_hi, hi_no[job])
                    for raw, h, l in a_of(job) if kind in ("at", "adt") else [parts(job)]:
                        ins = ve.tensor_tensor(l, raw, h.bitcast(F32), ALU.subtract)
                    ins.then_inc(s_lo, 1)

            def add_x2(t):
                ve.wait_ge(s_l1, t + 1)
                if t >= 3:
                    ve.wait_ge(s_x3, t - 2)
                ve.tensor_tensor(x2[:, t % 3, :], x1[:, t % 2, :], l1_of(t), ALU.add).then_inc(s_x2, 1)

            def low_x2t(t):
                ve.wait_ge(s_x2thi, t + 1)
                ve.tensor_tensor(x2t_hl[:, t % 2, 1, :, :], x2t_ps[:], x2t_hl[:, t % 2, 0, :, :].bitcast(F32),
                                 ALU.subtract).then_inc(s_x2tlo, 1)

            chain = [0]

            def link(ins):
                chain[0] += 1
                ins.then_inc(s_dve, 1)
                ve.wait_ge(s_dve, chain[0])

            def routing_parts(t):
                r = route[:, t % 2, :]
                return (r[:, 0:8], r[:, 8:16], r[:, 16:17], r[:, 17:18], r[:, 18:19], r[:, 19:20], r[:, 20:21],
                        r[:, 24:32], r[:, 32:40], r[:, 40:48])

            def route_top(t):
                logits, top, gap, _, _, _, _, ids, _, _ = routing_parts(t)
                ve.wait_ge(s_logits, t + 1)
                if t == 0:
                    ve.wait_ge(s_lang, 2)
                link(ve.tensor_tensor(logits, logits_of(t), lang5[:, t, :], ALU.add))
                link(ve.max(top, logits))
                ve.tensor_tensor(gap, top[:, 0:1], top[:, 1:2], ALU.subtract).then_inc(s_gap, 1)
                link(ve.max_index(order[:, t % 2, :], top, logits))
                link(ve.tensor_copy(ids, order[:, t % 2, :]))

            def route_gates(t):
                _, _, _, e, e1, w0, w1, ids, g0, g1 = routing_parts(t)
                ve.wait_ge(s_exp, t + 1)
                link(ve.tensor_scalar(e1, e, 1.0, 1.0 / SCALING, ALU.add, ALU.mult))
                link(ve.reciprocal(w0, e1))
                link(ve.tensor_tensor(w1, w0, e, ALU.mult))
                ve.tensor_scalar(g0, const("iota"), ids[:, 0:1], w0, ALU.is_equal, ALU.mult)
                link(ve.tensor_scalar(g1, const("iota"), ids[:, 1:2], w1, ALU.is_equal, ALU.mult))
                link(ve.tensor_tensor(g0, g0, g1, ALU.add))
                if t >= 2:
                    ve.wait_ge(s_hgt, t - 1)
                ve.wait_ge(s_base, t + 1)
                ve.tensor_tensor(hg[:, t % 2, :].rearrange("p (j e r) -> p j e r", j=2, r=RANK), h_of(t),
                                 g0.rearrange("p (j e) -> p j e", j=2).unsqueeze(3).to_broadcast(
                                     [P, 2, EXPERTS // 2, RANK]), ALU.mult).then_inc(s_hg, 1)

            def low_hgt(t):
                ve.wait_ge(s_hgthi, t + 1)
                ve.tensor_tensor(hgt_hl[:, t % 2, 1, :], hgt_ps[:, 0:P], hgt_hl[:, t % 2, 0, :].bitcast(F32),
                                 ALU.subtract).then_inc(s_hgtlo, 1)

            def add_x3(t):
                if t >= 3:
                    ve.wait_ge(s_y, t - 2)
                for n, (a, b) in enumerate(pieces(t)):
                    ve.wait_ge(s_l2, t + n + 1)
                    ve.tensor_tensor(halves(x3[:, t % 3, :], a, b), halves(x2[:, t % 3, :], a, b), base_of(t, a, b),
                                     ALU.add).then_inc(s_x3, 1)

            def low_last_x3():
                t = NT - 1
                for n, (a, b) in enumerate(pieces(t)):
                    ve.wait_ge(s_x3hi, t + n + 1)
                    ve.wait_ge(s_x3lo, t + n)
                    ve.tensor_tensor(x3_hl[:, t % 2, 1, a:b], x3[:, t % 3, a:b],
                                     x3_hl[:, t % 2, 0, a:b].bitcast(F32), ALU.subtract).then_inc(s_x3lo, 1)

            def add_y(t):
                if t >= 2:
                    ve.wait_ge(s_out[t % 2], 16 * (t // 2))
                for n, (a, b) in enumerate(pieces(t)):
                    ve.wait_ge(s_l3, t + n + 1)
                    ve.tensor_tensor(y[:, t % 2, a:b], x3[:, t % 3, a:b], l3_of(t, n),
                                     ALU.add).then_inc(s_y, 1)

            ve.memset(warm[:], 0.0).then_inc(s_warm, 1)
            ve.memset(td[:], 0.0).then_inc(s_zero, 1)
            batch_indices()
            for s in range(-1, STEPS + 2):
                for job in lane_jobs(s):
                    if job == ("at", 0, 0):
                        rank_indices()
                    job_lo(job)
                if s == STEPS:
                    add_x2(2)
                if s == STEPS + 1:
                    route_gates(0)
                if s == FC:
                    tile_indices()
                if 0 <= s - (STEPS - 5) <= HC:
                    n = s - (STEPS - 5)
                    ve.wait_ge(s_whi, n + 1)
                    raw, h, l = w2_parts(n)
                    ve.tensor_tensor(l, raw, h.bitcast(F32), ALU.subtract).then_inc(s_wlo, 1)
                if s == STEPS - 4:
                    ve.tensor_tensor(lang5[:], const("iota").unsqueeze(1).to_broadcast([P, NT, EXPERTS]),
                                     sel[:, 2, :].unsqueeze(2).to_broadcast([P, NT, EXPERTS]),
                                     ALU.is_equal).then_inc(s_lang, 1)
                    ve.wait_ge(s_lang, 1)
                    ve.tensor_scalar(lang5[:], lang5[:], LANG_BIAS, None, ALU.mult).then_inc(s_lang, 1)
                if s == STEPS - 3:
                    add_x2(0)
                if s == STEPS - 2:
                    add_x2(1)
                    low_x2t(0)
                if s == STEPS - 1:
                    low_x2t(1)

            for i in range(NT + 2):
                if 1 <= i <= NT:
                    low_hgt(i - 1)
                if i == NT:
                    add_y(NT - 3)
                if 1 <= i < NT:
                    route_top(i)
                if i == NT - 1:
                    route_gates(i)
                if 1 <= i and i + 1 < NT:
                    low_x2t(i + 1)
                if 1 <= i <= NT:
                    add_x3(i - 1)
                if i == NT:
                    low_last_x3()
                if 1 <= i < NT - 1:
                    route_gates(i)
                if 1 <= i and i + 2 < NT:
                    add_x2(i + 2)
                if i >= 2 and i != NT - 1:
                    add_y(i - 2)

        @block.tensor
        def _(pe):
            def product(out_, stationary, moving, start, stop):
                pe.matmul(out_, stationary[0], moving[0], start=start, stop=False, skip_group_check=True)
                pe.matmul(out_, stationary[0], moving[1], start=False, stop=False, skip_group_check=True)
                return pe.matmul(out_, stationary[1], moving[0], start=False, stop=stop, skip_group_check=True)

            def x_a(g, m):
                if m == 0:
                    pe.wait_ge(s_lo, s_lo_of(("x", g, 1)))
                pe.wait_ge(s_lo, s_lo_of(("at", g, m)))
                if m == 0 and g >= 1:
                    pe.wait_ge(s_mask, mask_no(("t", g - 1)))
                for c in range(HC):
                    a_t = agu_of(g, m)
                    mm = product(tg_ps[:, m, :], (a_t[:, 0, c, :], a_t[:, 1, c, :]),
                                 (xt[g % 2][:, 0, c, :], xt[g % 2][:, 1, c, :]), c == 0, c == HC - 1)
                mm.then_inc(s_tg, 1)

            def gate_up_base(s, m):
                g, f = divmod(s, FC)
                w = cw(f)
                if s >= GU_BANKS and m == 0:
                    pe.wait_ge(s_mul, s - GU_BANKS + 1)
                if s == STEPS - 1:
                    pe.wait_ge(s_x2, 1)
                if g == 0:
                    pe.wait_ge(s_lo, s_lo_of(("wgu", f, m)))
                for c in range(HC):
                    if f == 0 and m == 0 and c % (HC // 2) == 0:
                        pe.wait_ge(s_lo, s_lo_of(("x", g, c // (HC // 2))))
                    cols = slice(c * w, (c + 1) * w)
                    product(gu_ps[s % GU_BANKS][0:w, m, :], (wgu_at(f, m, 0)[:, cols], wgu_at(f, m, 1)[:, cols]),
                            (xt[g % 2][:, 0, c, :], xt[g % 2][:, 1, c, :]), m == 0 and c == 0, False)

            def gate_up_adapters(s):
                g, f = divmod(s, FC)
                w = cw(f)
                pe.wait_ge(s_lo, s_lo_of(("b", g, f // 2)))
                if f == 0:
                    pe.wait_ge(s_lo, s_lo_of(("t", g)))
                k = pair_at(g, f // 2) % 2
                for m in range(2):
                    at = f % 2 * 2 * P + m * w
                    cols = slice(at, at + w)
                    mm = product(gu_ps[s % GU_BANKS][0:w, m, :], (b_sel[:, k, 0, cols], b_sel[:, k, 1, cols]),
                                 (t_hl[:, g % 2, 0, m, :], t_hl[:, g % 2, 1, m, :]), False, m == 1)
                mm.then_inc(s_gu, 1)

            def down(s):
                g, f = divmod(s, FC)
                w = cw(f)
                pe.wait_ge(s_lo, s_lo_of(("act", s)))
                if g == 0:
                    pe.wait_ge(s_wdlo, f + 1)
                for n, (a, b) in enumerate(AD_PIECES):
                    if f == a:
                        pe.wait_ge(s_lo, s_lo_of(("adt", g, n)))
                if f == 0 and g >= 1:
                    pe.wait_ge(s_mask, mask_no(("td", g - 1)))
                for q in range(TILES):
                    if f == 0 and g >= 1:
                        pe.wait_ge(s_x1, TILES * (g - 1) + q + 1)
                    a_hl = [act_hl[0:w, s % 2, part, q * P:(q + 1) * P] for part in range(2)]
                    at = q * AD_HALF
                    for half in range(2):
                        mm = product(down_ps[q][:, half, 0:D_COLS], a_hl,
                                     [wd_sb[0:w, f, part, half, at:at + D_COLS] for part in range(2)], f == 0, False)
                mm.then_inc(s_d, 1)

            def transpose_td(g):
                pe.wait_ge(s_mask, mask_no(("td", g)))
                if g == NG - 1:
                    pe.wait_ge(s_x2tlo, 2)
                for q in range(TILES):
                    mm = pe.transpose(td_t[:, q * P:(q + 1) * P], td[:, q, :], ident)
                mm.then_inc(s_tdt, 1)

            def down_adapters(g):
                pe.wait_ge(s_lo, max(s_lo_of(("td", g)), s_lo_of(("bd", g))))
                for q in range(TILES):
                    rows = slice(q * P, (q + 1) * P)
                    for half in range(2):
                        cols = slice(half * HALF, (half + 1) * HALF)
                        mm = product(down_of(q)[:, half, :], (td_hl[:, 0, rows], td_hl[:, 1, rows]),
                                     (bd_hl[:, 0, cols], bd_hl[:, 1, cols]), False, True)
                    mm.then_inc(s_dl, 1)

            def mix(bank, t, m, x_hl):
                return product(bank, (bd13_hl[:, t % BD, 0, m, :], bd13_hl[:, t % BD, 1, m, :]),
                               (x_hl[:, t % 2, 0, :], x_hl[:, t % 2, 1, :]), True, True)

            def l1(t):
                pe.wait_ge(s_x1lo, t + 1)
                if t == 3:
                    pe.wait_ge(s_x1, TILES * NG)
                if t >= 1:
                    pe.wait_ge(s_x2, t)
                mix(l1_of(t), t, 0, x1_hl).then_inc(s_l1, 1)

            def transpose_x2(t):
                pe.wait_ge(s_x2, t + 1)
                if t >= 1:
                    pe.wait_ge(s_x2tlo, t)
                for c in range(HC):
                    mm = pe.transpose(x2t_ps[:, c, :], x2[:, t % 3, c * P:(c + 1) * P], ident)
                mm.then_inc(s_x2t, 1)

            def l2_base(t, half, c0=0, c1=HC):
                if half == 1:
                    pe.wait_ge(s_x2tlo, t + 1)
                    if t == 1:
                        pe.wait_ge(s_x1, TILES * (NG - 1) + 1)
                    if t >= 2:
                        pe.wait_ge(s_x3, t - 1)
                        pe.wait_ge(s_hg, t - 1)
                if t == 1 and half == 0 and c0 == 0:
                    pe.wait_ge(s_x2, 3)
                for c in range(c0, c1):
                    if t == 0 and half == 1:
                        pe.wait_ge(s_wlo, c + 1)
                    x_hl = x2t_hl[:, t % 2, 0, c, :], x2t_hl[:, t % 2, 1, c, :]
                    at, w = half * L2_WIDTH[0], L2_WIDTH[half]
                    mm = product(l2_ps[t % 2][:, half, 0:w], x_hl,
                                 [w2ra_hl[:, part, c, at:at + w] for part in range(2)], c == 0, c == HC - 1)
                if c1 == HC:
                    mm.then_inc((s_base, s_logits)[half], 1)

            def transpose_hg(t):
                pe.wait_ge(s_hg, t + 1)
                if t >= 1:
                    pe.wait_ge(s_hgtlo, t)
                pe.transpose(hgt_ps[:, 0:P], hg[:, t % 2, :], ident).then_inc(s_hgt, 1)

            def experts(t):
                pe.wait_ge(s_hgtlo, t + 1)
                if t == 0:
                    pe.wait_ge(s_wlo, HC + 1)
                for half in range(2):
                    cols = slice(half * HALF, (half + 1) * HALF)
                    mm = product(l2_ps[t % 2][:, half, 0:HALF], (hgt_hl[:, t % 2, 0, :], hgt_hl[:, t % 2, 1, :]),
                                 (b2_hl[:, 0, cols], b2_hl[:, 1, cols]), False, True)
                    if half == 1 or len(pieces(t)) == 2:
                        mm.then_inc(s_l2, 1)

            def l3(t):
                if t == NT - 1:
                    pe.wait_ge(s_x2, NT)
                    pe.wait_ge(s_hgtlo, NT)
                elif t >= 1:
                    pe.wait_ge(s_y, t)
                for n, (a, b) in enumerate(pieces(t)):
                    pe.wait_ge(s_x3lo, t + n + 1)
                    mix(l3_of(t, n), t, 1, x3_hl[:, :, :, a:b]).then_inc(s_l3, 1)

            for s in range(GU_BANKS - 1):
                for m in range(2):
                    gate_up_base(s, m)
            gate_up_base(GU_BANKS - 1, 0)
            x_a(0, 0)
            x_a(0, 1)
            gate_up_base(GU_BANKS - 1, 1)

            for s in range(STEPS):
                g, f = divmod(s, FC)
                if s >= GU_BANKS:
                    gate_up_base(s, 0)
                    if f == 1 and g > 0:
                        transpose_td(g - 1)
                    gate_up_base(s, 1)
                    if f == 1 and g > 0:
                        down_adapters(g - 1)
                gate_up_adapters(s)
                if s <= GU_BANKS:
                    if s >= 2:
                        down(s - 2)
                if s >= GU_BANKS:
                    down(s - 1)
                for n, m in x_a_jobs(s):
                    x_a(n, m)
                if s in (STEPS - 3, STEPS - 2):
                    l1(s - (STEPS - 3))
                if s in (STEPS - 2, STEPS - 1):
                    transpose_x2(s - (STEPS - 2))
            l2_base(0, 1)
            down(STEPS - 1)
            l2_base(0, 0, 0, HC // 2)
            transpose_td(NG - 1)
            l2_base(0, 0, HC // 2, HC)
            l1(2)
            down_adapters(NG - 1)
            for i in range(1, NT + 2):
                if i < NT:
                    l2_base(i, 1)
                if i - 1 < NT:
                    transpose_hg(i - 1)
                if i < NT:
                    l2_base(i, 0, 0, HC // 2)
                if i + 1 < NT:
                    transpose_x2(i + 1)
                if i < NT:
                    l2_base(i, 0, HC // 2, HC)
                if i - 1 < NT:
                    experts(i - 1)
                if i >= 2:
                    l3(i - 2)
                if i + 2 < NT:
                    l1(i + 2)

IDX_BATCH = 1
IDX_RANK = IDX_BATCH + 3
N_IDX = IDX_RANK + 3 + 2


def first_step(k):
    return k // PAIRS * FC + k % PAIRS * 2


def mask_no(job):
    order = [j for s in range(-1, STEPS + FC) for j in lane_jobs(s) if j[0] in ("t", "td")]
    return order.index(job) + 1


def kernel(**inputs):
    import concourse.bacc as bacc
    from concourse.bass_utils import run_bass_kernel_spmd

    a = {k: np.asarray(v) for k, v in inputs.items()}

    def chunked_t(w, width):
        t = w.T.reshape(HC, P, -1)
        return [t[:, :, c:c + width].transpose(1, 0, 2).reshape(P, -1) for c in range(0, t.shape[2], width)]

    rows = a["x"].reshape(ROWS, H)
    wgu = [m for pair in zip(chunked_t(a["L0_cond_W_gate"], P), chunked_t(a["L0_cond_W_up"], P)) for m in pair]
    ab = ADAPTERS * RANK
    b_gate, b_up = (a[f"L0_cond_B_{k}"][0].transpose(0, 2, 1).reshape(ab, F) for k in ("gate", "up"))
    a_down = np.zeros((ADAPTERS, RANK, FC * P), np.float32)
    a_down[:, :, :F] = a["L0_cond_A_down"][0]
    a_all = np.concatenate([m.reshape(ADAPTERS, RANK, -1, P).transpose(0, 3, 2, 1).reshape(ADAPTERS * P, -1)
                            for m in (a["L0_cond_A_gate"][0], a["L0_cond_A_up"][0], a_down)], axis=1)
    a_l2 = a["L2_cond_A"].reshape(EXPERTS * RANK, H)
    arrays = {
        "x_t": rows.T.reshape(HC, P, NG, GROUP).transpose(1, 2, 0, 3).reshape(P, NG, HC * GROUP),
        "x_rows": rows,
        "it_lora": a["itok_B_2_6"], "it_cond": a["itok_B_0_15"], "it_lang": a["itok_B_0_7"],
        "wgu": np.concatenate(wgu, axis=1),
        "wd": a["L0_cond_W_down"].T,
        "a_all": a_all,
        "b_d": a["L0_cond_B_down"][0].transpose(0, 2, 1).reshape(ab, H),
        "w13": np.concatenate([a["L1_cond_weights"], a["L3_cond_weights"]], axis=2).reshape(CONDS * CH, 2 * CH),
        "w2ra_t": np.concatenate([a["L2_cond_W"][:HALF], a_l2[:H_HALF], a["L2_cond_W"][HALF:], a_l2[H_HALF:],
                                  a["L2_cond_Wr"]]).T,
        "b2": a["L2_cond_B"].transpose(0, 2, 1).reshape(EXPERTS * RANK, H),
        "consts": CONSTS,
    }
    for n in range(PAIRS):
        chunks = [slice(c * P, c * P + cw(c)) for c in range(2 * n, min(2 * n + 2, FC))]
        arrays[f"b_gu{n}"] = np.concatenate([m[:, f] for f in chunks for m in (b_gate, b_up)], axis=1)
    arrays = {k: np.ascontiguousarray(v) for k, v in arrays.items()}

    nc = bacc.Bacc("TRN2", target_bir_lowering=False, num_devices=1)
    args = [nc.dram_tensor(k, v.shape, mybir.dt.from_np(v.dtype), kind="ExternalInput").ap()
            for k, v in arrays.items()]
    args.append(nc.dram_tensor("out", (ROWS, H), F32, kind="ExternalOutput").ap())
    bass_conditioned_residual_chain(nc, *args)
    r = run_bass_kernel_spmd(nc, [arrays], core_ids=[0])
    return r.results[0]["out"].reshape(BATCHES, CH, H)
```
